# Optimizing a Trainium2 kernel written in Bass

```python
import numpy as np
import jax
import jax.numpy as jnp

def _softmax(x, axis=-1):
    return jax.nn.softmax(x, axis=axis)

def _gelu(x):
    return jax.nn.gelu(x, approximate=True)

def _silu(x):
    return jax.nn.silu(x)

def _sigmoid(x):
    return jax.nn.sigmoid(x)

def _layernorm(x, axis=-1, eps=1e-05):
    m = jnp.mean(x, axis=axis, keepdims=True)
    v = jnp.var(x, axis=axis, keepdims=True)
    return (x - m) / jnp.sqrt(v + eps)

def _scatter_add(tgt, idx, src, axis=0):
    return tgt.at[idx].add(src)

def _segment_sum(src, seg, n):
    return jax.ops.segment_sum(src, seg, n)
kernel_name = 'mk_adj_preln_d1_adj_r2_d31cf9'

def setup_inputs(seed: int=0):
    np.random.seed(seed)
    _w = jnp.asarray

    def _rec_inputs():
        import jax
        import jax.numpy as jnp
        _gk = jax.random.key(seed)
        x = 7.22e-05 + 1 * jax.random.normal(jax.random.fold_in(_gk, 1), (32, 256, 512), jnp.float32)
        _w = (1.0 + jnp.arange(256, dtype=jnp.float32)) ** (-0.5)
        _w = _w / _w.mean()
        _pij = jnp.clip(0.03125 * _w[:, None] * _w[None, :], 0.0, 1.0)
        _a = jax.random.uniform(jax.random.fold_in(_gk, 2), (32, 256, 256)) < _pij
        _a = jnp.logical_or(_a, jnp.swapaxes(_a, -1, -2))
        _a = jnp.logical_or(_a, jnp.eye(256, dtype=bool))
        _af = _a.astype(jnp.float32)
        _af = _af * jax.random.uniform(jax.random.fold_in(_gk, 3), (32, 256, 256), jnp.float32, 0.05, 4.42607)
        adj = _af
        return (x, adj)
    x, adj = _rec_inputs()

    def _L0_gnn_setup():
        import jax, jax.numpy as jnp
        import numpy as np
        NUM_HEADS = 16
        key = jax.random.key(seed)
        ks = jax.random.split(key, 7)
        B, N, D = (16, 256, 512)
        return {'x': jax.random.normal(ks[0], (B, N, D), dtype=jnp.float32), 'spatial_encoding': jax.random.normal(ks[1], (B, N, N), dtype=jnp.float32), 'edge_encoding': jax.random.normal(ks[2], (B, N, N), dtype=jnp.float32), 'Wq': jax.random.normal(ks[3], (D, D), dtype=jnp.float32) * D ** (-0.5), 'Wk': jax.random.normal(ks[4], (D, D), dtype=jnp.float32) * D ** (-0.5), 'Wv': jax.random.normal(ks[5], (D, D), dtype=jnp.float32) * D ** (-0.5), 'Wo': jax.random.normal(ks[6], (D, D), dtype=jnp.float32) * D ** (-0.5)}
    _L0_gnn_all = _L0_gnn_setup()
    _L0_gnn_in = {k: v for k, v in _L0_gnn_all.items() if k in ('Wq', 'Wk', 'Wv', 'Wo')}
    del _L0_gnn_all
    return {'x': x, 'adj': adj, 'L0_gnn_Wq': _L0_gnn_in['Wq'], 'L0_gnn_Wk': _L0_gnn_in['Wk'], 'L0_gnn_Wv': _L0_gnn_in['Wv'], 'L0_gnn_Wo': _L0_gnn_in['Wo']}

def reference(x, adj, L0_gnn_Wq, L0_gnn_Wk, L0_gnn_Wv, L0_gnn_Wo):
    import jax
    import jax.numpy as jnp

    def _L0_gnn_ref(x, spatial_encoding, edge_encoding, Wq, Wk, Wv, Wo):
        import jax, jax.numpy as jnp
        import numpy as np
        NUM_HEADS = 16
        B, N, D = x.shape
        H = NUM_HEADS
        hd = D // H
        scale = D ** (-0.5)

        def split_heads(t):
            return t.reshape(B, N, H, hd).transpose(0, 2, 1, 3)
        q = split_heads(x @ Wq.T)
        k = split_heads(x @ Wk.T)
        v = split_heads(x @ Wv.T)
        bias = (spatial_encoding + edge_encoding)[:, None]
        a = jnp.einsum('bhnd,bhmd->bhnm', q, k) * scale + bias
        row_nonzero = jnp.any(a != 0, axis=-1, keepdims=True)
        a = jnp.where(row_nonzero, a, -jnp.inf)
        p = jax.nn.softmax(a, axis=-1)
        p = jnp.where(jnp.isnan(p), 0.0, p)
        o = jnp.einsum('bhnm,bhmd->bhnd', p, v)
        o = o.transpose(0, 2, 1, 3).reshape(B, N, D)
        return o @ Wo.T
    h = jnp.maximum(_layernorm(x, axis=-1), 0.0)
    x = x + _L0_gnn_ref(h, adj, adj, L0_gnn_Wq, L0_gnn_Wk, L0_gnn_Wv, L0_gnn_Wo)
    return x

_drawn_inputs = setup_inputs


def setup_inputs(seed=0):
    import zlib

    import numpy as np

    out = dict(_drawn_inputs(seed))
    spreads = {}
    factors = {'L0_gnn_Wq': 2.92, 'L0_gnn_Wk': 2.868}
    for name, (base, spread) in spreads.items():
        noise = np.random.default_rng([zlib.crc32(name.encode()), seed]).standard_normal(out[name].shape)
        drawn = base * np.exp(spread * noise) if base else spread * noise
        out[name] = jnp.asarray(drawn.astype(out[name].dtype))
    for name, factor in factors.items():
        out[name] = (out[name] * factor).astype(out[name].dtype)
    return out
```

```python
from contextlib import ExitStack

import concourse.bass as bass
from concourse import mybir

ALU = mybir.AluOpType
ACT = mybir.ActivationFunctionType
AX_X = mybir.AxisListType.X
F32 = mybir.dt.float32
F32R = mybir.dt.float32r
F16 = mybir.dt.float16
BF16 = mybir.dt.bfloat16

P = 128
HEADS = 16
EPS = 1e-5
GREATEST = 3.4e38

WHOLE, HEAD, TAIL = "whole", "head", "tail"
JOBS = {
    0: [("qk", 3, 0, HEAD)],
    1: [("qk", 3, 0, TAIL), ("o", 3, -1, WHOLE)],
    2: [("v", 2, 0, WHOLE)],
    3: [("v", 3, 0, WHOLE)],
    4: [("y", 0, -1, HEAD)],
    5: [("y", 0, -1, TAIL), ("h", 0, 1, WHOLE)],
    6: [("y", 1, -1, HEAD)],
    7: [("y", 1, -1, TAIL), ("h", 1, 1, WHOLE)],
    8: [("o", 0, 0, WHOLE), ("qk", 0, 1, HEAD)],
    9: [("qk", 0, 1, TAIL)],
    10: [("v", 0, 1, WHOLE)],
    11: [("v", 1, 1, WHOLE), ("o", 1, 0, WHOLE)],
    12: [("qk", 1, 1, HEAD)],
    13: [("qk", 1, 1, TAIL), ("o", 2, 0, WHOLE)],
    14: [("qk", 2, 1, HEAD)],
    15: [("qk", 2, 1, TAIL)],
}
ORDER = [(kind, n) for hh in range(HEADS) for kind, n, _, part in JOBS[hh] if part != TAIL]
BANK = {job: i % 2 for i, job in enumerate(ORDER)}
FIRST_JOBS = [("h", 0), ("h", 1), ("qk", 0), ("v", 0), ("v", 1), ("qk", 1), ("qk", 2)]
PER_BATCH = {"h": 2, "qk": 4, "v": 4, "o": 4, "y": 2}


def jobs_at(hh, first, last):
    return [j for j in JOBS[hh] if not (first and j[2] < 0) and not (last and j[2] > 0)]


def ended_before(hh, first, last):
    if hh:
        return [j[:3] for j in jobs_at(hh - 1, first, last) if j[3] != HEAD]
    return [(kind, n, d - 1) for kind, n, d, part in JOBS[HEADS - 1] if part != HEAD]


def attention_block(nc, x, adj, wq_t, wk_t, wv_t, wo_t, out):
    B, N, D = x.shape
    NT = N // P
    KT = D // P
    HD = D // HEADS
    G = P // HD
    HALF = D // 2
    HH = HEADS // 2
    VW = 3 * HD + 2
    VN = 3 * HD + 1
    PAIRS = HEADS // 2
    HALF_SCALE = 0.5 * float(D) ** -0.5
    STACKS = 3 * G
    SPLIT = 16 * STACKS
    assert NT == 2 and KT == 4 and G == 4 and HD == 32

    x_d = x.rearrange("b (t p) d -> b p t d", p=P)
    adj_d = adj.rearrange("b (t p) m -> b p t m", p=P)
    out_d = out.rearrange("b (t p) d -> b p t d", p=P)

    with ExitStack() as ctx:
        def sb(name, shape, dt=F32):
            return ctx.enter_context(nc.sbuf_tensor(name, shape, dt))

        def psum(name):
            return ctx.enter_context(nc.psum_tensor(name, [P, 512], F32))

        def sem(name):
            return ctx.enter_context(nc.semaphore(name))

        w_hi = [sb(f"w_hi{i}", [P, KT, D], F32R) for i in range(4)]
        w_lo = [sb(f"w_lo{i}", [P, KT, D], F32R) for i in range(4)]
        WQ, WK, WV, WO = range(4)
        x_in = sb("x_in", [P, NT, D])
        x_res = sb("x_res", [P, NT, D])
        h = sb("h", [P, NT, D])
        w_in = [x_in, x_res, h, sb("y", [P, NT, D])]
        y = w_in[3]
        hT_hi = sb("hT_hi", [P, KT, N], F32R)
        hT_lo = sb("hT_lo", [P, KT, N], F32R)
        qk_parts = [sb(f"qk_parts{i}", [P, 4, N], F32R) for i in range(2)]
        qk_stack = sb("qk_stack", [3 * HD, HEADS, 2, N], F32R)
        v_parts = sb("v_parts", [P, NT, HEADS, VW], BF16)
        v_rest = [sb(f"v_rest{i}", [P, HALF]) for i in range(2)]
        adj_in = sb("adj_in", [P, NT, N])
        adj_now = sb("adj_now", [P, NT, N])
        minus = [sb(f"minus{i}", [P, 2, NT, N]) for i in range(2)]
        minus_max = sb("minus_max", [P, 4, 2, NT])
        fold1 = [sb(f"fold1_{i}", [P, 2 * NT, N // 2]) for i in range(2)]
        fold2 = [sb(f"fold2_{i}", [P, 2 * NT, N // 4]) for i in range(2)]
        some = sb("some", [P, 4, 2 * NT])
        probs = [sb(f"probs{i}", [P, NT, N]) for i in range(2)]
        pT_hi = [sb(f"pT_hi{i}", [P, NT, N], F16) for i in range(2)]
        pT_lo = [sb(f"pT_lo{i}", [P, NT, N], F16) for i in range(2)]
        o_sum = sb("o_sum", [P, 2 * NT, HD])
        o = sb("o", [P, NT, D])
        oT_hi = sb("oT_hi", [P, KT, N], F32R)
        oT_lo = sb("oT_lo", [P, KT, N], F32R)
        stats = sb("stats", [P, NT, 6])
        mean_var = sb("mean_var", [P, NT, 2])
        var_eps = sb("var_eps", [P, NT])
        minus_half = sb("minus_half", [P, NT])
        rstd = sb("rstd", [P, NT])
        ident = sb("ident", [P, P])

        s_ps = [psum(f"s_ps{i}") for i in range(2)]
        pT_ps = [psum(f"pT_ps{i}") for i in range(2)]
        o_ps = [psum(f"o_ps{i}") for i in range(2)]
        job_ps = [psum(f"job_ps{i}") for i in range(2)]

        w_loaded = [sem(f"w_loaded{i}") for i in range(4)]
        w_high = sem("w_high")
        w_split = sem("w_split")
        ident_zero, constants = sem("ident_zero"), sem("constants")
        x_loaded, adj_loaded, res_loaded = sem("x_loaded"), sem("adj_loaded"), sem("res_loaded")
        adj_copied = sem("adj_copied")
        stats_done, moments = sem("stats_done"), sem("moments")
        eps_added, rstd_ready, h_ready = sem("eps_added"), sem("rstd_ready"), sem("h_ready")
        ended = {k: sem(f"ended_{k}") for k in PER_BATCH}
        high = {k: sem(f"high_{k}") for k in PER_BATCH if k != "y"}
        taken = {k: sem(f"taken_{k}") for k in PER_BATCH}
        v_mid, v_done = sem("v_mid"), sem("v_done")
        stacked = [sem(f"stacked{i}") for i in range(2)]
        scores_ready, shifted, exp_done = sem("scores_ready"), sem("shifted"), sem("exp_done")
        pT_ready, pT_high, pT_split = sem("pT_ready"), sem("pT_high"), sem("pT_split")
        pv_done, folded1, folded2 = sem("pv_done"), sem("folded1"), sem("folded2")
        o_added, some_ready, keep_ready = sem("o_added"), sem("some_ready"), sem("keep_ready")
        rcp_ready, factor_ready, o_ready = sem("rcp_ready"), sem("factor_ready"), sem("o_ready")
        stored = [sem(f"stored{i}") for i in range(NT)]

        went_on = {e: sem(f"went_on_{e}") for e in ("dve", "pool", "sp")}

        block = ctx.enter_context(nc.Block())

        def settled(engine, name):
            engine.sem_inc(went_on[name], 1)

        def count(kind, n, b):
            return b * PER_BATCH[kind] + (n + 1)

        def head_no(b, hh):
            return b * HEADS + hh

        def stack_count(g, b):
            return b * (2 * SPLIT) + SPLIT * (g // 2 + 1)

        @block.sync
        def _(sp):
            def stack(g, b, first):
                sp.wait_ge(taken["qk"], count("qk", g, b))
                settled(sp, "sp")
                if not first:
                    sp.wait_ge(scores_ready, head_no(b, 0) + (G * g + G - HEADS))
                    settled(sp, "sp")
                parts = qk_parts[g % 2]
                for r, pair in enumerate((slice(1, 3), slice(0, 3, 2), slice(1, 4, 2))):
                    for j in range(G):
                        sp.dma_start(qk_stack[HD * r:HD * (r + 1), G * g + j, :, :].bitcast(F32),
                                     parts[HD * j:HD * (j + 1), pair, :].bitcast(F32)
                                     ).then_inc(stacked[g % 2], 16)

            def load_weight(i, w):
                dst = w_in[i]
                w_v = w.rearrange("(k p) n -> p k n", p=P)
                return dst, w_v

            for i, w in enumerate((wq_t, wk_t, wv_t, wo_t)):
                dst, w_v = load_weight(i, w)
                sp.dma_start(dst[:, :, :], w_v[:, 0:2, :]).then_inc(w_loaded[i], 16)
            for i, w in enumerate((wq_t, wk_t, wv_t, wo_t)):
                dst, w_v = load_weight(i, w)
                sp.wait_ge(w_split, i + 1)
                sp.dma_start(dst[:, :, :], w_v[:, 2:4, :]).then_inc(w_loaded[i], 16)
            sp.wait_ge(w_split, 5)
            sp.dma_start(x_in[:, :, :], x_d[0]).then_inc(x_loaded, 16)
            sp.dma_start(adj_in[:, :, :], adj_d[0]).then_inc(adj_loaded, 16)
            sp.wait_ge(w_split, 6)
            sp.dma_start(x_res[:, :, :], x_d[0]).then_inc(res_loaded, 16)
            for g in range(3):
                stack(g, 0, True)

            def body(b, first, last):
                if not last:
                    sp.wait_ge(h_ready, b + 1)
                    settled(sp, "sp")
                    sp.dma_start(x_in[:, :, :], x_d[b + 1]).then_inc(x_loaded, 16)
                    sp.wait_ge(adj_copied, b + 1)
                    settled(sp, "sp")
                    sp.dma_start(adj_in[:, :, :], adj_d[b + 1]).then_inc(adj_loaded, 16)
                stack(3, b, first)
                if not first:
                    store(b - 1)
                    sp.dma_start(x_res[:, :, :], x_d[b]).then_inc(res_loaded, 16)
                if not last:
                    for g in range(3):
                        stack(g, b + 1, False)

            def store(b):
                for t in range(NT):
                    sp.wait_ge(taken["y"], count("y", t, b))
                    settled(sp, "sp")
                    sp.dma_start(out_d[b, :, t, :], y[:, t, :]).then_inc(stored[t], 16)

            body(0, True, False)
            with sp.Fori(1, B - 1) as b:
                body(b, False, False)
            body(B - 1, False, True)
            store(B - 1)
            for t in range(NT):
                sp.wait_ge(stored[t], 16 * B)

        @block.tensor
        def _(pe):
            last_in = {}

            def begin(kind, n, d, b):
                bank = BANK[kind, n]
                if bank in last_in:
                    was, m, e = last_in[bank]
                    pe.wait_ge(taken[was], count(was, m, b + e))
                last_in[bank] = (kind, n, d)
                return job_ps[bank]

            def product(dst, lhs, rhs):
                terms = [(k, a, c) for k in range(KT) for a, c in ((0, 0), (0, 1), (1, 0))]
                for i, (k, a, c) in enumerate(terms):
                    end = nc.tensor.matmul(dst, lhs[a](k), rhs[c](k), start=i == 0, stop=i == len(terms) - 1)
                return end

            hT = (hT_hi, hT_lo)

            def job(kind, n, d, part, b):
                if part != TAIL:
                    ps = begin(kind, n, d, b)
                else:
                    ps = job_ps[BANK[kind, n]]
                if kind == "h":
                    if n == 0:
                        pe.wait_ge(h_ready, b + (d + 1))
                    for k in range(2):
                        for t in range(NT):
                            end = nc.tensor.transpose(ps[:, k * N + t * P:k * N + (t + 1) * P],
                                                      h[:, t, (2 * n + k) * P:(2 * n + k + 1) * P], ident[:, :])
                    end.then_inc(ended["h"], 1)
                elif kind == "qk":
                    if n == 0 and part != TAIL:
                        pe.wait_ge(taken["h"], count("h", 1, b + d))
                    i = WK if part == TAIL else WQ
                    dst = ps[:, N:2 * N] if part == TAIL else ps[:, 0:N]
                    end = product(dst, [lambda k, w=w: w[:, k, n * P:(n + 1) * P] for w in (w_hi[i], w_lo[i])],
                                  [lambda k, v=v: v[:, k, :] for v in hT])
                    if part == TAIL:
                        end.then_inc(ended["qk"], 1)
                elif kind == "v":
                    t, half = n % NT, n // NT
                    end = product(ps[:, 0:HALF], [lambda k, v=v: v[:, k, t * P:(t + 1) * P] for v in hT],
                                  [lambda k, w=w: w[:, k, half * HALF:(half + 1) * HALF] for w in (w_hi[WV], w_lo[WV])])
                    end.then_inc(ended["v"], 1)
                elif kind == "o":
                    pe.wait_ge(o_ready, (b + d) * PAIRS + 2 * (n + 1))
                    for t in range(NT):
                        end = nc.tensor.transpose(ps[:, t * P:(t + 1) * P], o[:, t, n * P:(n + 1) * P], ident[:, :])
                    end.then_inc(ended["o"], 1)
                else:
                    if n == 0 and part != TAIL:
                        pe.wait_ge(taken["o"], count("o", 3, b + d))
                    terms = [(k, a, c) for k in range(KT) for a, c in ((0, 0), (0, 1), (1, 0))]
                    cut = len(terms) // 2
                    for i, (k, a, c) in enumerate(terms):
                        if (part == TAIL) == (i >= cut):
                            end = nc.tensor.matmul(ps[:, :], (oT_hi, oT_lo)[a][:, k, n * P:(n + 1) * P],
                                                   (w_hi, w_lo)[c][WO][:, k, :], start=i == 0,
                                                   stop=i == len(terms) - 1)
                    if part == TAIL:
                        end.then_inc(ended["y"], 1)

            def scores(b, hh, early=False):
                if hh % G == 0:
                    g = hh // G
                    pe.wait_ge(stacked[g % 2], stack_count(g, b))
                if not early:
                    pe.wait_ge(shifted, head_no(b, hh) - 1)
                for t in range(NT):
                    end = nc.tensor.matmul(s_ps[hh % 2][:, t * N:(t + 1) * N], qk_stack[:, hh, 0, t * P:(t + 1) * P],
                                           qk_stack[:, hh, 1, :], start=True, stop=True)
                end.then_inc(scores_ready, 1)

            def transpose_probs(b, hh, early):
                pe.wait_ge(exp_done, head_no(b, hh) + 1)
                if not early:
                    pe.wait_ge(pT_split, head_no(b, hh) - 1)
                for m in range(NT):
                    for t in range(NT):
                        end = nc.tensor.transpose(pT_ps[hh % 2][:, m * N + t * P:m * N + (t + 1) * P],
                                                  probs[hh % 2][:, t, m * P:(m + 1) * P], ident[:, :])
                end.then_inc(pT_ready, 1)

            def values(b, hh, early):
                if hh % HH == 0:
                    pe.wait_ge(v_done, count("v", 2 * (hh // HH) + 1, b))
                if hh % 2 == 0 and not early:
                    pe.wait_ge(o_ready, b * PAIRS + (hh // 2 - 1))
                pe.wait_ge(pT_split, head_no(b, hh) + 1)
                for t in range(NT):
                    q = (hh % 2) * NT + t
                    dst = o_ps[hh // 2 % 2][:, q * P:q * P + VN]
                    terms = [(m, a) for m in range(NT) for a in range(2)]
                    for i, (m, a) in enumerate(terms):
                        end = nc.tensor.matmul(dst, (pT_hi, pT_lo)[a][hh % 2][:, m, t * P:(t + 1) * P],
                                               v_parts[:, m, hh, 0:VN], start=i == 0, stop=i == len(terms) - 1)
                end.then_inc(pv_done, 1)

            pe.wait_ge(constants, 3)
            pe.wait_ge(w_split, 8)
            for kind, n in FIRST_JOBS:
                if kind == "qk":
                    job(kind, n, 0, HEAD, 0)
                    job(kind, n, 0, TAIL, 0)
                else:
                    job(kind, n, 0, WHOLE, 0)
            for hh in range(2):
                scores(0, hh, True)

            def body(b, first, last):
                for hh in range(HEADS):
                    if hh + 2 < HEADS:
                        scores(b, hh + 2)
                    elif not last:
                        scores(b + 1, hh + 2 - HEADS)
                    transpose_probs(b, hh, first and hh < 2)
                    if hh:
                        values(b, hh - 1, first and hh - 1 < 4)
                    elif not first:
                        values(b - 1, HEADS - 1, False)
                    for kind, n, d, part in jobs_at(hh, first, last):
                        job(kind, n, d, part, b)
                for bank, (kind, n, d) in last_in.items():
                    last_in[bank] = (kind, n, d - 1)

            body(0, True, False)
            with pe.Fori(1, B - 1) as b:
                body(b, False, False)
            body(B - 1, False, True)
            values(B - 1, HEADS - 1, False)
            job("o", 3, -1, WHOLE, B)
            for n in range(NT):
                job("y", n, -1, HEAD, B)
                job("y", n, -1, TAIL, B)

        @block.scalar
        def _(act):
            for part in range(2):
                for i in range(4):
                    act.wait_ge(w_loaded[i], 16 * (part + 1))
                    nc.scalar.activation(w_hi[i][:, 2 * part:2 * part + 2, :], w_in[i][:, :, :],
                                         ACT.Copy).then_inc(w_high, 1)

            def take(kind, n, b, early=False):
                ps = job_ps[BANK[kind, n]]
                if kind == "y":
                    return
                if kind == "qk":
                    if not (early and n < 2):
                        was = (n - 2, b) if n >= 2 else (n + 2, b - 1)
                        act.wait_ge(stacked[n % 2], stack_count(*was))
                act.wait_ge(ended[kind], count(kind, n, b))
                if kind == "h":
                    nc.scalar.activation(hT_hi[:, 2 * n:2 * n + 2, :], ps[:, :].rearrange("p (k n) -> p k n", k=2),
                                         ACT.Relu).then_inc(high["h"], 1)
                elif kind == "qk":
                    nc.scalar.activation(qk_parts[n % 2][:, 1, :], ps[:, 0:N], ACT.Copy, scale=HALF_SCALE)
                    nc.scalar.activation(qk_parts[n % 2][:, 2, :], ps[:, N:2 * N], ACT.Copy).then_inc(high["qk"], 1)
                elif kind == "v":
                    t, half = n % NT, n // NT
                    if not early:
                        act.wait_ge(pv_done, head_no(b, 0) + (HH * (half + 1) - HEADS))
                    nc.scalar.activation(v_parts[:, t, half * HH:(half + 1) * HH, 0:HD],
                                         ps[:, 0:HALF].rearrange("p (h d) -> p h d", d=HD),
                                         ACT.Copy).then_inc(high["v"], 1)
                elif kind == "o":
                    nc.scalar.activation(oT_hi[:, n, :], ps[:, 0:N], ACT.Copy).then_inc(high["o"], 1)

            def exponentials(b, hh, early):
                act.wait_ge(shifted, head_no(b, hh) + 1)
                if not early:
                    act.wait_ge(pT_ready, head_no(b, hh) - 1)
                for t in range(NT):
                    end = nc.scalar.activation(probs[hh % 2][:, t, :], minus[hh // 2 % 2][:, hh % 2, t, :], ACT.Exp,
                                               bias=minus_max[:, hh // 2 % 4, hh % 2, t:t + 1], scale=-1.0)
                end.then_inc(exp_done, 1)

            def high_probs(b, hh, early):
                act.wait_ge(pT_ready, head_no(b, hh) + 1)
                if not early:
                    act.wait_ge(pv_done, head_no(b, hh) - 1)
                nc.scalar.activation(pT_hi[hh % 2][:, :, :], pT_ps[hh % 2][:, :].rearrange("p (m n) -> p m n", m=NT),
                                     ACT.Copy).then_inc(pT_high, 1)

            for kind, n in FIRST_JOBS[:-1]:
                take(kind, n, 0, True)
            exponentials(0, 0, True)

            def body(b, first, last):
                for hh in range(HEADS):
                    if hh + 1 < HEADS:
                        exponentials(b, hh + 1, first and hh + 1 < 2)
                    elif not last:
                        exponentials(b + 1, 0, False)
                    for kind, n, d in ended_before(hh, first, last):
                        take(kind, n, b + d, first and (kind, d) in (("v", 0), ("qk", 0)))
                    high_probs(b, hh, first and hh < 2)

            body(0, True, False)
            with act.Fori(1, B - 1) as b:
                body(b, False, False)
            body(B - 1, False, True)
            take("o", 3, B - 1)

        @block.vector
        def _(dve):
            for part in range(2):
                for i in range(4):
                    dve.wait_ge(w_high, 4 * part + i + 1)
                    nc.vector.tensor_tensor(w_lo[i][:, 2 * part:2 * part + 2, :], w_in[i][:, :, :],
                                            w_hi[i][:, 2 * part:2 * part + 2, :].bitcast(F32),
                                            ALU.subtract).then_inc(w_split, 1)

            def moments_of(b):
                dve.wait_ge(x_loaded, (b + 1) * 16)
                for t in range(NT):
                    end = nc.vector.bn_stats(stats[:, t, :], x_in[:, t, :])
                end.then_inc(stats_done, 1)
                dve.wait_ge(stats_done, b + 1)
                settled(dve, "dve")
                for t in range(NT):
                    end = nc.vector.bn_aggr(mean_var[:, t, :], stats[:, t, :])
                end.then_inc(moments, 1)

            def normalise(b, first):
                dve.wait_ge(rstd_ready, b + 1)
                if not first:
                    dve.wait_ge(ended["h"], b * 2)
                for t in range(NT):
                    end = nc.vector.tensor_scalar(h[:, t, :], x_in[:, t, :], mean_var[:, t, 0:1], rstd[:, t:t + 1],
                                                  ALU.subtract, ALU.mult)
                end.then_inc(h_ready, 1)

            def take(kind, n, b):
                ps = job_ps[BANK[kind, n]]
                if kind != "y":
                    dve.wait_ge(high[kind], count(kind, n, b))
                if kind == "h":
                    nc.vector.scalar_tensor_tensor(hT_lo[:, 2 * n:2 * n + 2, :].rearrange("p k n -> p (k n)"),
                                                   ps[:, :], 0.0,
                                                   hT_hi[:, 2 * n:2 * n + 2, :].bitcast(F32).rearrange("p k n -> p (k n)"),
                                                   ALU.max, ALU.subtract).then_inc(taken["h"], 1)
                elif kind == "qk":
                    parts = qk_parts[n % 2]
                    nc.vector.scalar_tensor_tensor(parts[:, 0, :], ps[:, 0:N], HALF_SCALE,
                                                   parts[:, 1, :].bitcast(F32), ALU.mult, ALU.subtract)
                    nc.vector.tensor_tensor(parts[:, 3, :], ps[:, N:2 * N], parts[:, 2, :].bitcast(F32),
                                            ALU.subtract).then_inc(taken["qk"], 1)
                elif kind == "v":
                    t, half = n % NT, n // NT
                    if not (isinstance(b, int) and b == 0 and n < 2):
                        dve.wait_ge(v_done, count("v", n, b) - 2)
                    nc.vector.tensor_tensor(v_rest[n % 2][:, :].rearrange("p (h d) -> p h d", d=HD),
                                            ps[:, 0:HALF].rearrange("p (h d) -> p h d", d=HD),
                                            v_parts[:, t, half * HH:(half + 1) * HH, 0:HD],
                                            ALU.subtract).then_inc(taken["v"], 1)
                elif kind == "o":
                    nc.vector.tensor_tensor(oT_lo[:, n, :], ps[:, 0:N], oT_hi[:, n, :].bitcast(F32),
                                            ALU.subtract).then_inc(taken["o"], 1)
                else:
                    if n == 0:
                        dve.wait_ge(res_loaded, (b + 1) * 16)
                    if not (isinstance(b, int) and b == 0):
                        dve.wait_ge(stored[n], b * 16)
                    dve.wait_ge(ended["y"], count("y", n, b))
                    nc.vector.tensor_tensor(y[:, n, :], ps[:, :], x_res[:, n, :], ALU.add).then_inc(taken["y"], 1)

            def shift(b, hh, early):
                pair = hh // 2
                if hh % 2 == 0 and not early:
                    dve.wait_ge(folded1, b * PAIRS + (pair - 1))
                    dve.wait_ge(exp_done, head_no(b, hh) - 2)
                dve.wait_ge(scores_ready, head_no(b, hh) + 1)
                settled(dve, "dve")
                for t in range(NT):
                    end = nc.vector.tensor_tensor_reduce(
                        out=minus[pair % 2][:, hh % 2, t, :], in0=s_ps[hh % 2][:, t * N:(t + 1) * N],
                        in1=adj_now[:, t, :], scale=-2.0, scalar=GREATEST, op0=ALU.add, op1=ALU.min,
                        accum_out=minus_max[:, pair % 4, hh % 2, t:t + 1])
                end.then_inc(shifted, 1)

            def copy_adj(b):
                dve.wait_ge(adj_loaded, (b + 1) * 16)
                if not (isinstance(b, int) and b == 0):
                    dve.wait_ge(shifted, head_no(b, 0))
                nc.vector.tensor_copy(adj_now[:, :, :], adj_in[:, :, :]).then_inc(adj_copied, 1)
                dve.wait_ge(adj_copied, b + 1)

            def low_probs(b, hh, early):
                dve.wait_ge(pT_high, head_no(b, hh) + 1)
                nc.vector.tensor_tensor(pT_lo[hh % 2][:, :, :], pT_ps[hh % 2][:, :].rearrange("p (m n) -> p m n", m=NT),
                                        pT_hi[hh % 2][:, :, :], ALU.subtract).then_inc(pT_split, 1)

            def outputs(b, pair, first):
                no = b * PAIRS + (pair + 1)
                ps = o_ps[pair % 2][:, :].rearrange("p (q c) -> p q c", c=P)
                dve.wait_ge(folded2, no)
                nc.vector.tensor_reduce(some[:, 0, :], fold2[pair % 2][:, :, :], AX_X, ALU.add).then_inc(some_ready, 1)
                dve.wait_ge(pv_done, head_no(b, 2 * pair + 2))
                nc.vector.tensor_reduce(o_sum[:, :, :], ps[:, :, 0:3 * HD].rearrange("p q (j d) -> p q d j", j=3),
                                        AX_X, ALU.add).then_inc(o_added, 1)
                nc.vector.reciprocal(some[:, 1, :], ps[:, :, 3 * HD]).then_inc(rcp_ready, 1)
                dve.wait_ge(some_ready, no)
                nc.vector.scalar_tensor_tensor(some[:, 2, :],
                                               minus_max[:, pair % 4, :, :].rearrange("p h t -> p (h t)"), 0.0,
                                               some[:, 0, :], ALU.not_equal, ALU.max).then_inc(keep_ready, 1)
                dve.wait_ge(rcp_ready, no)
                dve.wait_ge(keep_ready, no)
                nc.vector.scalar_tensor_tensor(some[:, 3, :], some[:, 2, :], 0.0, some[:, 1, :],
                                               ALU.not_equal, ALU.mult).then_inc(factor_ready, 1)
                dve.wait_ge(factor_ready, no)
                dve.wait_ge(o_added, no)
                for k in range(2):
                    col = (2 * pair + k) * HD
                    end = nc.vector.tensor_tensor(
                        o[:, :, col:col + HD], o_sum[:, k * NT:(k + 1) * NT, :],
                        some[:, 3, k * NT:(k + 1) * NT].unsqueeze(2).to_broadcast([P, NT, HD]), ALU.mult)
                end.then_inc(o_ready, 1)

            moments_of(0)
            normalise(0, True)
            for kind, n in FIRST_JOBS[:-1]:
                take(kind, n, 0)
            copy_adj(0)
            for hh in range(2):
                shift(0, hh, True)

            def body(b, first, last):
                for hh in range(HEADS):
                    if hh + 2 < HEADS:
                        shift(b, hh + 2, first and hh + 2 < 4)
                    elif not last:
                        if hh + 2 == HEADS:
                            copy_adj(b + 1)
                        shift(b + 1, hh + 2 - HEADS, False)
                    for kind, n, d in ended_before(hh, first, last):
                        take(kind, n, b + d)
                    low_probs(b, hh, first and hh < 2)
                    if not last and hh == 1:
                        moments_of(b + 1)
                    if not last and hh == 3:
                        normalise(b + 1, False)
                    if hh % 2 == 0 and hh:
                        outputs(b, hh // 2 - 1, first)
                    elif hh == 0 and not first:
                        outputs(b - 1, PAIRS - 1, False)

            body(0, True, False)
            with dve.Fori(1, B - 1) as b:
                body(b, False, False)
            body(B - 1, False, True)
            outputs(B - 1, PAIRS - 1, False)
            take("o", 3, B - 1)
            for n in range(NT):
                take("y", n, B - 1)

        @block.gpsimd
        def _(pool):
            nc.gpsimd.memset(ident[:, :], 0.0).then_inc(ident_zero, 1)
            pool.wait_ge(ident_zero, 1)
            nc.gpsimd.affine_select(out=ident[:, :], in_=ident[:, :], compare_op=ALU.not_equal, fill=1.0, base=0,
                                    pattern=[[-1, P]], channel_multiplier=1).then_inc(constants, 1)
            nc.gpsimd.memset(minus_half[:, :], -0.5).then_inc(constants, 1)
            nc.gpsimd.memset(v_parts[:, :, :, 3 * HD:VW], 1.0).then_inc(constants, 1)

            def deviations(b):
                pool.wait_ge(moments, b + 1)
                settled(pool, "pool")
                nc.gpsimd.tensor_scalar(var_eps[:, :], mean_var[:, :, 1], EPS, None, ALU.add).then_inc(eps_added, 1)
                pool.wait_ge(eps_added, b + 1)
                nc.gpsimd.tensor_tensor(rstd[:, :], var_eps[:, :], minus_half[:, :], ALU.pow).then_inc(rstd_ready, 1)

            def values(n, b):
                t, half = n % NT, n // NT
                rest = v_rest[n % 2][:, :].rearrange("p (h d) -> p h d", d=HD)
                mid = v_parts[:, t, half * HH:(half + 1) * HH, HD:2 * HD]
                pool.wait_ge(taken["v"], count("v", n, b))
                settled(pool, "pool")
                nc.gpsimd.tensor_copy(mid, rest).then_inc(v_mid, 1)
                pool.wait_ge(v_mid, count("v", n, b))
                nc.gpsimd.tensor_tensor(v_parts[:, t, half * HH:(half + 1) * HH, 2 * HD:3 * HD], rest, mid,
                                        ALU.subtract).then_inc(v_done, 1)

            def fold(b, pair, early):
                src = minus[pair % 2][:, :, :, :].rearrange("p h t n -> p (h t) n")
                f1, f2 = fold1[pair % 2], fold2[pair % 2]
                pool.wait_ge(shifted, head_no(b, 2 * pair + 2))
                nc.gpsimd.tensor_tensor(f1[:, :, :], src[:, :, 0:N // 2], src[:, :, N // 2:N],
                                        ALU.add).then_inc(folded1, 1)
                pool.wait_ge(folded1, b * PAIRS + (pair + 1))
                if not early:
                    pool.wait_ge(some_ready, b * PAIRS + (pair - 1))
                nc.gpsimd.tensor_tensor(f2[:, :, :], f1[:, :, 0:N // 4], f1[:, :, N // 4:N // 2],
                                        ALU.add).then_inc(folded2, 1)

            deviations(0)
            values(0, 0)
            values(1, 0)
            fold(0, 0, True)

            def body(b, first, last):
                for hh in range(HEADS):
                    for kind, n, d in ended_before(hh, first, last):
                        if kind == "v":
                            values(n, b + d)
                    if not last and hh == 1:
                        deviations(b + 1)
                    if hh % 2 == 1:
                        if hh + 2 < HEADS:
                            fold(b, hh // 2 + 1, first and hh // 2 + 1 < 2)
                        elif not last:
                            fold(b + 1, 0, False)

            body(0, True, False)
            with pool.Fori(1, B - 1) as b:
                body(b, False, False)
            body(B - 1, False, True)


_OUT = (32, 256, 512)


def kernel(x, adj, L0_gnn_Wq, L0_gnn_Wk, L0_gnn_Wv, L0_gnn_Wo):
    import numpy as np
    import concourse.bacc as bacc
    from concourse import mybir
    from concourse.bass_utils import run_bass_kernel_spmd

    laid_out = {
        "x": np.ascontiguousarray(x),
        "adj": np.ascontiguousarray(adj),
        "wq_t": np.ascontiguousarray(np.asarray(L0_gnn_Wq).T),
        "wk_t": np.ascontiguousarray(np.asarray(L0_gnn_Wk).T),
        "wv_t": np.ascontiguousarray(np.asarray(L0_gnn_Wv).T),
        "wo_t": np.ascontiguousarray(np.asarray(L0_gnn_Wo).T),
    }
    nc = bacc.Bacc("TRN2", target_bir_lowering=False, num_devices=1)
    args = [nc.dram_tensor(name, a.shape, mybir.dt.from_np(a.dtype), kind="ExternalInput").ap()
            for name, a in laid_out.items()]
    out = nc.dram_tensor("out", _OUT, mybir.dt.float32, kind="ExternalOutput").ap()
    attention_block(nc, *args, out)
    got = run_bass_kernel_spmd(nc, [laid_out], core_ids=[0])
    return got.results[0]["out"]
```

```python
from contextlib import ExitStack

import concourse.bass as bass
from concourse import mybir

ALU = mybir.AluOpType
ACT = mybir.ActivationFunctionType
AX_X = mybir.AxisListType.X
F32 = mybir.dt.float32
F32R = mybir.dt.float32r
F16 = mybir.dt.float16
I32 = mybir.dt.int32

P = 128
HEADS = 16
EPS = 1e-5
GREATEST = 3.4e38
EXPONENT = 0x7F800000
LEAST_SCALE = 2.0 ** -100

WHOLE, HEAD, TAIL = "whole", "head", "tail"
JOBS = {
    0: [("qk", 3, 0, HEAD)],
    1: [("qk", 3, 0, TAIL)],
    2: [("v", 2, 0, WHOLE), ("o", 3, -1, WHOLE)],
    3: [("v", 3, 0, WHOLE)],
    4: [("y", 0, -1, HEAD)],
    5: [("y", 0, -1, TAIL), ("h", 0, 1, WHOLE)],
    6: [("y", 1, -1, HEAD)],
    7: [("y", 1, -1, TAIL), ("h", 1, 1, WHOLE)],
    8: [("o", 0, 0, WHOLE), ("qk", 0, 1, HEAD)],
    9: [("qk", 0, 1, TAIL)],
    10: [("v", 0, 1, WHOLE)],
    11: [("v", 1, 1, WHOLE), ("o", 1, 0, WHOLE)],
    12: [("qk", 1, 1, HEAD)],
    13: [("qk", 1, 1, TAIL)],
    14: [("qk", 2, 1, HEAD)],
    15: [("qk", 2, 1, TAIL), ("o", 2, 0, WHOLE)],
}
ORDER = [(kind, n) for hh in range(HEADS) for kind, n, _, part in JOBS[hh] if part != TAIL]
BANK = {job: i % 2 for i, job in enumerate(ORDER)}
FIRST_JOBS = [("h", 0), ("h", 1), ("qk", 0), ("v", 0), ("v", 1), ("qk", 1), ("qk", 2)]
PER_BATCH = {"h": 2, "qk": 4, "v": 4, "o": 4, "y": 2}


def jobs_at(hh, first, last):
    return [j for j in JOBS[hh] if not (first and j[2] < 0) and not (last and j[2] > 0)]


def ended_before(hh, first, last):
    if hh:
        return [j[:3] for j in jobs_at(hh - 1, first, last) if j[3] != HEAD]
    return [(kind, n, d - 1) for kind, n, d, part in JOBS[HEADS - 1] if part != HEAD and not (first and d < 1)]


def attention_block(nc, x, adj, wq_t, wk_t, wv, wo_t, out):
    B, N, D = x.shape
    NT = N // P
    KT = D // P
    HD = D // HEADS
    G = P // HD
    HALF = D // 2
    HH = HEADS // 2
    VW = 2 * HD + 2
    ONES, LOW = HD, HD + 1
    PAIRS = HEADS // 2
    HALF_SCALE = 0.5 * float(D) ** -0.5
    STACKS = 3 * G
    SPLIT = 16 * STACKS
    assert NT == 2 and KT == 4 and G == 4 and HD == 32

    x_d = x.rearrange("b (t p) d -> b p t d", p=P)
    adj_d = adj.rearrange("b (t p) m -> b p t m", p=P)
    out_d = out.rearrange("b (t p) d -> b p t d", p=P)

    with ExitStack() as ctx:
        def sb(name, shape, dt=F32):
            return ctx.enter_context(nc.sbuf_tensor(name, shape, dt))

        def psum(name):
            return ctx.enter_context(nc.psum_tensor(name, [P, 512], F32))

        def sem(name):
            return ctx.enter_context(nc.semaphore(name))

        w_hi = [sb(f"w_hi{i}", [P, KT, D], F32R) for i in range(4)]
        w_lo = [sb(f"w_lo{i}", [P, KT, D], F32R) for i in range(4)]
        WQ, WK, WV, WO = range(4)
        SPLITS = (WQ, WK, WV, WO)
        x_in = sb("x_in", [P, NT, D])
        x_res = sb("x_res", [P, NT, D])
        h = sb("h", [P, NT, D])
        w_in = [x_in, x_res, h, sb("y", [P, NT, D])]
        y = w_in[3]
        hT_hi = sb("hT_hi", [P, KT, N], F32R)
        hT_lo = sb("hT_lo", [P, KT, N], F32R)
        qk_parts = [sb(f"qk_parts{i}", [P, 4, N], F32R) for i in range(2)]
        qk_stack = sb("qk_stack", [3 * HD, HEADS, 2, N], F32R)
        v_parts = sb("v_parts", [P, NT, HEADS, VW], F16)
        adj_in = sb("adj_in", [P, NT, N])
        adj_now = sb("adj_now", [P, NT, N])
        minus = [sb(f"minus{i}", [P, 2, NT, N]) for i in range(2)]
        minus_max = sb("minus_max", [P, 4, 2, NT])
        fold1 = [sb(f"fold1_{i}", [P, 2 * NT, N // 2]) for i in range(2)]
        fold2 = [sb(f"fold2_{i}", [P, 2 * NT, N // 4]) for i in range(2)]
        fold3 = [sb(f"fold3_{i}", [P, 2 * NT, N // 8]) for i in range(2)]
        some = sb("some", [P, 4, 2 * NT])
        probs = [sb(f"probs{i}", [P, NT, N]) for i in range(2)]
        pT_hi = [sb(f"pT_hi{i}", [P, NT, N], F16) for i in range(2)]
        pT_lo = [sb(f"pT_lo{i}", [P, NT, N], F16) for i in range(2)]
        o = sb("o", [P, NT, D])
        oT_hi = sb("oT_hi", [P, KT, N], F32R)
        oT_lo = sb("oT_lo", [P, KT, N], F32R)
        v_scale = sb("v_scale", [P, 4, KT])
        stats = sb("stats", [P, NT, 6])
        mean_var = sb("mean_var", [P, NT, 2])
        var_eps = sb("var_eps", [P, NT])
        minus_half = sb("minus_half", [P, NT])
        rstd = sb("rstd", [P, NT])
        ident = sb("ident", [P, P])

        s_ps = [psum(f"s_ps{i}") for i in range(2)]
        pT_ps = [psum(f"pT_ps{i}") for i in range(2)]
        o_ps = [psum(f"o_ps{i}") for i in range(2)]
        job_ps = [psum(f"job_ps{i}") for i in range(2)]
        v_ps = [pT_ps, s_ps]

        w_loaded = [sem(f"w_loaded{i}") for i in range(4)]
        w_high = sem("w_high")
        w_split = sem("w_split")
        ident_zero, constants = sem("ident_zero"), sem("constants")
        x_loaded, adj_loaded, res_loaded = sem("x_loaded"), sem("adj_loaded"), sem("res_loaded")
        adj_copied = sem("adj_copied")
        stats_done, moments = sem("stats_done"), sem("moments")
        eps_added, rstd_ready, h_ready = sem("eps_added"), sem("rstd_ready"), sem("h_ready")
        ended = {k: sem(f"ended_{k}") for k in PER_BATCH}
        high = {k: sem(f"high_{k}") for k in PER_BATCH if k != "y"}
        taken = {k: sem(f"taken_{k}") for k in PER_BATCH}
        v_extent = sem("v_extent")
        v_scaled, v_turned, scale_ready = sem("v_scaled"), sem("v_turned"), sem("scale_ready")
        o_scaled = sem("o_scaled")
        stacked = [sem(f"stacked{i}") for i in range(2)]
        scores_ready, shifted, exp_done = sem("scores_ready"), sem("shifted"), sem("exp_done")
        pT_ready, pT_high, pT_split = sem("pT_ready"), sem("pT_high"), sem("pT_split")
        pv_done, folded1 = sem("pv_done"), sem("folded1")
        folded2, folded3 = sem("folded2"), sem("folded3")
        some_ready, keep_ready = sem("some_ready"), sem("keep_ready")
        rcp_ready, factor_ready, o_ready = sem("rcp_ready"), sem("factor_ready"), sem("o_ready")
        stored = [sem(f"stored{i}") for i in range(NT)]

        went_on = {e: sem(f"went_on_{e}") for e in ("dve", "pool", "sp")}

        block = ctx.enter_context(nc.Block())

        def settled(engine, name):
            engine.sem_inc(went_on[name], 1)

        def count(kind, n, b):
            return b * PER_BATCH[kind] + (n + 1)

        def head_no(b, hh):
            return b * HEADS + hh

        def stack_count(g, b):
            return b * (2 * SPLIT) + SPLIT * (g // 2 + 1)

        @block.sync
        def _(sp):
            def stack(g, b, first):
                sp.wait_ge(taken["qk"], count("qk", g, b))
                settled(sp, "sp")
                if not first:
                    sp.wait_ge(scores_ready, head_no(b, 0) + (G * g + G - HEADS))
                    settled(sp, "sp")
                parts = qk_parts[g % 2]
                for r, pair in enumerate((slice(1, 3), slice(0, 3, 2), slice(1, 4, 2))):
                    for j in range(G):
                        sp.dma_start(qk_stack[HD * r:HD * (r + 1), G * g + j, :, :].bitcast(F32),
                                     parts[HD * j:HD * (j + 1), pair, :].bitcast(F32)
                                     ).then_inc(stacked[g % 2], 16)

            def load_tokens(b):
                sp.wait_ge(h_ready, b)
                settled(sp, "sp")
                sp.dma_start(x_in[:, :, :], x_d[b]).then_inc(x_loaded, 16)

            for half in range(2):
                for i, w in ((WV, wv), (WQ, wq_t), (WK, wk_t), (WO, wo_t)):
                    if half:
                        if i == WV:
                            sp.wait_ge(v_turned, 1)
                        else:
                            sp.wait_ge(w_split, SPLITS.index(i) + 1)
                    sp.dma_start(w_in[i][:, :, :], w.rearrange("(k p) n -> p k n", p=P)[:, 2 * half:2 * half + 2, :]
                                 ).then_inc(w_loaded[i], 16)
            sp.wait_ge(w_split, 4 + SPLITS.index(WQ) + 1)
            sp.dma_start(x_in[:, :, :], x_d[0]).then_inc(x_loaded, 16)
            sp.dma_start(adj_in[:, :, :], adj_d[0]).then_inc(adj_loaded, 16)
            sp.wait_ge(w_split, 4 + SPLITS.index(WK) + 1)
            sp.dma_start(x_res[:, :, :], x_d[0]).then_inc(res_loaded, 16)
            load_tokens(1)
            for g in range(3):
                stack(g, 0, True)

            def body(b, first, last):
                if not last:
                    sp.wait_ge(adj_copied, b + 1)
                    settled(sp, "sp")
                    sp.dma_start(adj_in[:, :, :], adj_d[b + 1]).then_inc(adj_loaded, 16)
                stack(3, b, first)
                if not (last or isinstance(b, int) and b + 2 == B):
                    load_tokens(b + 2)
                if not first:
                    store(b - 1)
                    sp.dma_start(x_res[:, :, :], x_d[b]).then_inc(res_loaded, 16)
                if not last:
                    for g in range(3):
                        stack(g, b + 1, False)

            def store(b):
                for t in range(NT):
                    sp.wait_ge(taken["y"], count("y", t, b))
                    settled(sp, "sp")
                    sp.dma_start(out_d[b, :, t, :], y[:, t, :]).then_inc(stored[t], 16)

            body(0, True, False)
            with sp.Fori(1, B - 2) as b:
                body(b, False, False)
            body(B - 2, False, False)
            body(B - 1, False, True)
            store(B - 1)
            for t in range(NT):
                sp.wait_ge(stored[t], 16 * B)

        @block.tensor
        def _(pe):
            last_in = {}

            def begin(kind, n, d, b):
                bank = BANK[kind, n]
                if bank in last_in:
                    was, m, e = last_in[bank]
                    pe.wait_ge(taken[was], count(was, m, b + e))
                last_in[bank] = (kind, n, d)
                return job_ps[bank]

            def product(dst, lhs, rhs):
                terms = [(k, a, c) for k in range(KT) for a, c in ((0, 0), (0, 1), (1, 0))]
                for i, (k, a, c) in enumerate(terms):
                    end = nc.tensor.matmul(dst, lhs[a](k), rhs[c](k), start=i == 0, stop=i == len(terms) - 1)
                return end

            hT = (hT_hi, hT_lo)

            def job(kind, n, d, part, b):
                if part != TAIL:
                    ps = begin(kind, n, d, b)
                else:
                    ps = job_ps[BANK[kind, n]]
                if kind == "h":
                    if n == 0:
                        pe.wait_ge(h_ready, b + (d + 1))
                    for k in range(2):
                        for t in range(NT):
                            end = nc.tensor.transpose(ps[:, k * N + t * P:k * N + (t + 1) * P],
                                                      h[:, t, (2 * n + k) * P:(2 * n + k + 1) * P], ident[:, :])
                    end.then_inc(ended["h"], 1)
                elif kind == "qk":
                    if n == 0 and part != TAIL:
                        pe.wait_ge(taken["h"], count("h", 1, b + d))
                    i = WK if part == TAIL else WQ
                    dst = ps[:, N:2 * N] if part == TAIL else ps[:, 0:N]
                    end = product(dst, [lambda k, w=w: w[:, k, n * P:(n + 1) * P] for w in (w_hi[i], w_lo[i])],
                                  [lambda k, v=v: v[:, k, :] for v in hT])
                    if part == TAIL:
                        end.then_inc(ended["qk"], 1)
                elif kind == "v":
                    t, half = n % NT, n // NT
                    end = product(ps[:, 0:HALF], [lambda k, v=v: v[:, k, t * P:(t + 1) * P] for v in hT],
                                  [lambda k, w=w: w[:, k, half * HALF:(half + 1) * HALF] for w in (w_hi[WV], w_lo[WV])])
                    end.then_inc(ended["v"], 1)
                elif kind == "o":
                    pe.wait_ge(o_ready, (b + d) * PAIRS + 2 * (n + 1))
                    for t in range(NT):
                        end = nc.tensor.transpose(ps[:, t * P:(t + 1) * P], o[:, t, n * P:(n + 1) * P], ident[:, :])
                    end.then_inc(ended["o"], 1)
                else:
                    if n == 0 and part != TAIL:
                        pe.wait_ge(taken["o"], count("o", 3, b + d))
                    terms = [(k, a, c) for k in range(KT) for a, c in ((0, 0), (0, 1), (1, 0))]
                    cut = len(terms) // 2
                    for i, (k, a, c) in enumerate(terms):
                        if (part == TAIL) == (i >= cut):
                            end = nc.tensor.matmul(ps[:, :], (oT_hi, oT_lo)[a][:, k, n * P:(n + 1) * P],
                                                   (w_hi, w_lo)[c][WO][:, k, :], start=i == 0,
                                                   stop=i == len(terms) - 1)
                    if part == TAIL:
                        end.then_inc(ended["y"], 1)

            def scores(b, hh, early=False):
                if hh % G == 0:
                    g = hh // G
                    pe.wait_ge(stacked[g % 2], stack_count(g, b))
                if not early:
                    pe.wait_ge(shifted, head_no(b, hh) - 1)
                for t in range(NT):
                    end = nc.tensor.matmul(s_ps[hh % 2][:, t * N:(t + 1) * N], qk_stack[:, hh, 0, t * P:(t + 1) * P],
                                           qk_stack[:, hh, 1, :], start=True, stop=True)
                end.then_inc(scores_ready, 1)

            def transpose_probs(b, hh, early):
                pe.wait_ge(exp_done, head_no(b, hh) + 1)
                if not early:
                    pe.wait_ge(pT_split, head_no(b, hh) - 1)
                for m in range(NT):
                    for t in range(NT):
                        end = nc.tensor.transpose(pT_ps[hh % 2][:, m * N + t * P:m * N + (t + 1) * P],
                                                  probs[hh % 2][:, t, m * P:(m + 1) * P], ident[:, :])
                end.then_inc(pT_ready, 1)

            def values(b, hh, early):
                if hh % HH == 0:
                    pe.wait_ge(taken["v"], count("v", 2 * (hh // HH) + 1, b))
                if hh % 2 == 0 and not early:
                    pe.wait_ge(o_ready, b * PAIRS + (hh // 2 - 1))
                pe.wait_ge(pT_split, head_no(b, hh) + 1)
                for t in range(NT):
                    q = (hh % 2) * NT + t
                    ps = o_ps[hh // 2 % 2][:, q * P:(q + 1) * P]
                    for m in range(NT):
                        hi = pT_hi[hh % 2][:, m, t * P:(t + 1) * P]
                        lo = pT_lo[hh % 2][:, m, t * P:(t + 1) * P]
                        v = v_parts[:, m, hh, :]
                        nc.tensor.matmul(ps[:, 0:HD + 1], hi, v[:, 0:HD + 1], start=m == 0, stop=False)
                        nc.tensor.matmul(ps[:, 0:HD], hi, v[:, LOW:LOW + HD], start=False, stop=False)
                        end = nc.tensor.matmul(ps[:, 0:HD + 1], lo, v[:, 0:HD + 1], start=False, stop=m == NT - 1)
                end.then_inc(pv_done, 1)

            pe.wait_ge(constants, 3)
            for half in range(2):
                pe.wait_ge(v_scaled, half + 1)
                for k in range(KT):
                    for t in range(2):
                        col = (k % 2) * HALF + t * P
                        end = nc.tensor.transpose(v_ps[half][k // 2][:, col:col + P],
                                                  w_in[WV][:, t, k * P:(k + 1) * P], ident[:, :])
                end.then_inc(v_turned, 1)
            pe.wait_ge(w_split, 8)
            for kind, n in FIRST_JOBS:
                if kind == "qk":
                    job(kind, n, 0, HEAD, 0)
                    job(kind, n, 0, TAIL, 0)
                else:
                    job(kind, n, 0, WHOLE, 0)
            for hh in range(2):
                scores(0, hh, True)

            def body(b, first, last):
                for hh in range(HEADS):
                    if hh + 2 < HEADS:
                        scores(b, hh + 2)
                    elif not last:
                        scores(b + 1, hh + 2 - HEADS)
                    transpose_probs(b, hh, first and hh < 2)
                    if hh:
                        values(b, hh - 1, first and hh - 1 < 4)
                    elif not first:
                        values(b - 1, HEADS - 1, False)
                    for kind, n, d, part in jobs_at(hh, first, last):
                        job(kind, n, d, part, b)
                for bank, (kind, n, d) in last_in.items():
                    last_in[bank] = (kind, n, d - 1)

            body(0, True, False)
            with pe.Fori(1, B - 1) as b:
                body(b, False, False)
            body(B - 1, False, True)
            values(B - 1, HEADS - 1, False)
            job("o", 3, -1, WHOLE, B)
            for n in range(NT):
                job("y", n, -1, HEAD, B)
                job("y", n, -1, TAIL, B)

        @block.scalar
        def _(act):
            for half in range(2):
                part = slice(2 * half, 2 * half + 2)
                for i in SPLITS:
                    if i == WV:
                        act.wait_ge(v_turned, half + 1)
                        for j in range(2):
                            end = nc.scalar.activation(w_hi[WV][:, 2 * j:2 * j + 2, half * HALF:(half + 1) * HALF],
                                                       v_ps[half][j][:, :].rearrange("p (k n) -> p k n", k=2), ACT.Copy)
                        end.then_inc(w_high, 1)
                        continue
                    if i == WO:
                        act.wait_ge(o_scaled, half + 1)
                    else:
                        act.wait_ge(w_loaded[i], 16 * (half + 1))
                    nc.scalar.activation(w_hi[i][:, part, :], w_in[i][:, :, :], ACT.Copy).then_inc(w_high, 1)

            def take(kind, n, b, early=False):
                ps = job_ps[BANK[kind, n]]
                if kind == "y":
                    return
                if kind == "qk":
                    if not (early and n < 2):
                        was = (n - 2, b) if n >= 2 else (n + 2, b - 1)
                        act.wait_ge(stacked[n % 2], stack_count(*was))
                act.wait_ge(ended[kind], count(kind, n, b))
                if kind == "h":
                    nc.scalar.activation(hT_hi[:, 2 * n:2 * n + 2, :], ps[:, :].rearrange("p (k n) -> p k n", k=2),
                                         ACT.Relu).then_inc(high["h"], 1)
                elif kind == "qk":
                    nc.scalar.activation(qk_parts[n % 2][:, 1, :], ps[:, 0:N], ACT.Copy, scale=HALF_SCALE)
                    nc.scalar.activation(qk_parts[n % 2][:, 2, :], ps[:, N:2 * N], ACT.Copy).then_inc(high["qk"], 1)
                elif kind == "v":
                    t, half = n % NT, n // NT
                    if not early:
                        act.wait_ge(pv_done, head_no(b, 0) + (HH * (half + 1) - HEADS))
                    nc.scalar.activation(v_parts[:, t, half * HH:(half + 1) * HH, 0:HD],
                                         ps[:, 0:HALF].rearrange("p (h d) -> p h d", d=HD),
                                         ACT.Copy).then_inc(high["v"], 1)
                elif kind == "o":
                    nc.scalar.activation(oT_hi[:, n, :], ps[:, 0:N], ACT.Copy).then_inc(high["o"], 1)

            def exponentials(b, hh, early):
                act.wait_ge(shifted, head_no(b, hh) + 1)
                if not early:
                    act.wait_ge(pT_ready, head_no(b, hh) - 1)
                for t in range(NT):
                    end = nc.scalar.activation(probs[hh % 2][:, t, :], minus[hh // 2 % 2][:, hh % 2, t, :], ACT.Exp,
                                               bias=minus_max[:, hh // 2 % 4, hh % 2, t:t + 1], scale=-1.0)
                end.then_inc(exp_done, 1)

            def high_probs(b, hh, early):
                act.wait_ge(pT_ready, head_no(b, hh) + 1)
                if not early:
                    act.wait_ge(pv_done, head_no(b, hh) - 1)
                nc.scalar.activation(pT_hi[hh % 2][:, :, :], pT_ps[hh % 2][:, :].rearrange("p (m n) -> p m n", m=NT),
                                     ACT.Copy).then_inc(pT_high, 1)

            for kind, n in FIRST_JOBS[:-1]:
                take(kind, n, 0, True)
            exponentials(0, 0, True)

            def body(b, first, last):
                for hh in range(HEADS):
                    if hh + 1 < HEADS:
                        exponentials(b, hh + 1, first and hh + 1 < 2)
                    elif not last:
                        exponentials(b + 1, 0, False)
                    for kind, n, d in ended_before(hh, first, last):
                        take(kind, n, b + d, first and (kind, d) in (("v", 0), ("qk", 0)))
                    high_probs(b, hh, first and hh < 2)

            body(0, True, False)
            with act.Fori(1, B - 1) as b:
                body(b, False, False)
            body(B - 1, False, True)
            take("o", 2, B - 1)
            take("o", 3, B - 1)

        @block.vector
        def _(dve):
            for half in range(2):
                part = slice(2 * half, 2 * half + 2)
                dve.wait_ge(w_loaded[WV], 16 * (half + 1))
                nc.vector.tensor_reduce(v_scale[:, 0, part], w_in[WV][:, :, :], AX_X, ALU.max)
                nc.vector.tensor_reduce(v_scale[:, 1, part], w_in[WV][:, :, :], AX_X, ALU.min).then_inc(v_extent, 1)
                dve.wait_ge(v_extent, 5 * half + 1)
                nc.vector.scalar_tensor_tensor(v_scale[:, 2, part], v_scale[:, 1, part], -1.0, v_scale[:, 0, part],
                                               ALU.mult, ALU.max).then_inc(v_extent, 1)
                dve.wait_ge(v_extent, 5 * half + 2)
                nc.vector.tensor_scalar(v_scale[:, 3, part], v_scale[:, 2, part], LEAST_SCALE, None,
                                        ALU.max).then_inc(v_extent, 1)
                dve.wait_ge(v_extent, 5 * half + 3)
                nc.vector.tensor_scalar(v_scale[:, 2, part].bitcast(I32), v_scale[:, 3, part].bitcast(I32),
                                        EXPONENT, None, ALU.bitwise_and).then_inc(v_extent, 1)
                dve.wait_ge(v_extent, 5 * half + 4)
                nc.vector.reciprocal(v_scale[:, 3, part], v_scale[:, 2, part]).then_inc(v_extent, 1)
                dve.wait_ge(v_extent, 5 * half + 5)
                for k in range(2):
                    end = nc.vector.tensor_scalar(w_in[WV][:, k, :], w_in[WV][:, k, :],
                                                  v_scale[:, 3, 2 * half + k:2 * half + k + 1], None, ALU.mult)
                end.then_inc(v_scaled, 1)
                dve.wait_ge(w_loaded[WO], 16 * (half + 1))
                for k in range(2):
                    end = nc.vector.tensor_scalar(w_in[WO][:, k, :], w_in[WO][:, k, :],
                                                  v_scale[:, 2, 2 * half + k:2 * half + k + 1], None, ALU.mult)
                end.then_inc(o_scaled, 1)
                for n, i in enumerate(SPLITS):
                    dve.wait_ge(w_high, 4 * half + n + 1)
                    if i == WV:
                        for j in range(2):
                            cols = slice(half * HALF, (half + 1) * HALF)
                            end = nc.vector.tensor_tensor(
                                w_lo[WV][:, 2 * j:2 * j + 2, cols],
                                v_ps[half][j][:, :].rearrange("p (k n) -> p k n", k=2),
                                w_hi[WV][:, 2 * j:2 * j + 2, cols].bitcast(F32), ALU.subtract)
                    else:
                        end = nc.vector.tensor_tensor(w_lo[i][:, part, :], w_in[i][:, :, :],
                                                      w_hi[i][:, part, :].bitcast(F32), ALU.subtract)
                    end.then_inc(w_split, 1)

            def moments_of(b):
                dve.wait_ge(x_loaded, (b + 1) * 16)
                for t in range(NT):
                    end = nc.vector.bn_stats(stats[:, t, :], x_in[:, t, :])
                end.then_inc(stats_done, 1)
                dve.wait_ge(stats_done, b + 1)
                settled(dve, "dve")
                for t in range(NT):
                    end = nc.vector.bn_aggr(mean_var[:, t, :], stats[:, t, :])
                end.then_inc(moments, 1)

            def normalise(b, first):
                dve.wait_ge(rstd_ready, b + 1)
                if not first:
                    dve.wait_ge(ended["h"], b * 2)
                for t in range(NT):
                    end = nc.vector.tensor_scalar(h[:, t, :], x_in[:, t, :], mean_var[:, t, 0:1], rstd[:, t:t + 1],
                                                  ALU.subtract, ALU.mult)
                end.then_inc(h_ready, 1)

            def take(kind, n, b):
                ps = job_ps[BANK[kind, n]]
                if kind != "y":
                    dve.wait_ge(high[kind], count(kind, n, b))
                if kind == "h":
                    nc.vector.scalar_tensor_tensor(hT_lo[:, 2 * n:2 * n + 2, :].rearrange("p k n -> p (k n)"),
                                                   ps[:, :], 0.0,
                                                   hT_hi[:, 2 * n:2 * n + 2, :].bitcast(F32).rearrange("p k n -> p (k n)"),
                                                   ALU.max, ALU.subtract).then_inc(taken["h"], 1)
                elif kind == "qk":
                    parts = qk_parts[n % 2]
                    nc.vector.scalar_tensor_tensor(parts[:, 0, :], ps[:, 0:N], HALF_SCALE,
                                                   parts[:, 1, :].bitcast(F32), ALU.mult, ALU.subtract)
                    nc.vector.tensor_tensor(parts[:, 3, :], ps[:, N:2 * N], parts[:, 2, :].bitcast(F32),
                                            ALU.subtract).then_inc(taken["qk"], 1)
                elif kind == "v":
                    t, half = n % NT, n // NT
                    part = v_parts[:, t, half * HH:(half + 1) * HH, :]
                    nc.vector.tensor_tensor(part[:, :, LOW:LOW + HD],
                                            ps[:, 0:HALF].rearrange("p (h d) -> p h d", d=HD), part[:, :, 0:HD],
                                            ALU.subtract).then_inc(taken["v"], 1)
                elif kind == "o":
                    nc.vector.tensor_tensor(oT_lo[:, n, :], ps[:, 0:N], oT_hi[:, n, :].bitcast(F32),
                                            ALU.subtract).then_inc(taken["o"], 1)
                else:
                    if n == 0:
                        dve.wait_ge(res_loaded, (b + 1) * 16)
                    if not (isinstance(b, int) and b == 0):
                        dve.wait_ge(stored[n], b * 16)
                    dve.wait_ge(ended["y"], count("y", n, b))
                    nc.vector.tensor_tensor(y[:, n, :], ps[:, :], x_res[:, n, :], ALU.add).then_inc(taken["y"], 1)

            def shift(b, hh, early):
                pair = hh // 2
                if hh % 2 == 0 and not early:
                    dve.wait_ge(folded1, b * PAIRS + (pair - 1))
                    dve.wait_ge(exp_done, head_no(b, hh) - 2)
                dve.wait_ge(scores_ready, head_no(b, hh) + 1)
                settled(dve, "dve")
                for t in range(NT):
                    end = nc.vector.tensor_tensor_reduce(
                        out=minus[pair % 2][:, hh % 2, t, :], in0=s_ps[hh % 2][:, t * N:(t + 1) * N],
                        in1=adj_now[:, t, :], scale=-2.0, scalar=GREATEST, op0=ALU.add, op1=ALU.min,
                        accum_out=minus_max[:, pair % 4, hh % 2, t:t + 1])
                end.then_inc(shifted, 1)

            def copy_adj(b):
                dve.wait_ge(adj_loaded, (b + 1) * 16)
                if not (isinstance(b, int) and b == 0):
                    dve.wait_ge(shifted, head_no(b, 0))
                nc.vector.tensor_copy(adj_now[:, :, :], adj_in[:, :, :]).then_inc(adj_copied, 1)
                dve.wait_ge(adj_copied, b + 1)

            def low_probs(b, hh, early):
                dve.wait_ge(pT_high, head_no(b, hh) + 1)
                nc.vector.tensor_tensor(pT_lo[hh % 2][:, :, :], pT_ps[hh % 2][:, :].rearrange("p (m n) -> p m n", m=NT),
                                        pT_hi[hh % 2][:, :, :], ALU.subtract).then_inc(pT_split, 1)

            def divide1(b, pair):
                dve.wait_ge(folded3, b * PAIRS + (pair + 1))
                nc.vector.tensor_reduce(some[:, 0, :], fold3[pair % 2][:, :, :], AX_X, ALU.add).then_inc(some_ready, 1)
                dve.wait_ge(pv_done, head_no(b, 2 * pair + 2))
                nc.vector.reciprocal(some[:, 1, :],
                                     o_ps[pair % 2][:, :].rearrange("p (q c) -> p q c", c=P)[:, :, ONES]
                                     ).then_inc(rcp_ready, 1)

            def divide2(b, pair):
                dve.wait_ge(some_ready, b * PAIRS + (pair + 1))
                nc.vector.scalar_tensor_tensor(some[:, 2, :],
                                               minus_max[:, pair % 4, :, :].rearrange("p h t -> p (h t)"), 0.0,
                                               some[:, 0, :], ALU.not_equal, ALU.max).then_inc(keep_ready, 1)

            def divide3(b, pair):
                dve.wait_ge(rcp_ready, b * PAIRS + (pair + 1))
                dve.wait_ge(keep_ready, b * PAIRS + (pair + 1))
                nc.vector.scalar_tensor_tensor(some[:, 3, :], some[:, 2, :], 0.0, some[:, 1, :],
                                               ALU.not_equal, ALU.mult).then_inc(factor_ready, 1)

            def divide4(b, pair):
                dve.wait_ge(factor_ready, b * PAIRS + (pair + 1))
                col = 2 * pair * HD
                nc.vector.tensor_tensor(
                    o[:, :, col:col + 2 * HD].rearrange("p t (h d) -> p h t d", h=2),
                    o_ps[pair % 2][:, :].rearrange("p (h t c) -> p h t c", h=2, c=P)[:, :, :, 0:HD],
                    some[:, 3, :].rearrange("p (h t) -> p h t", h=2).unsqueeze(3).to_broadcast([P, 2, NT, HD]),
                    ALU.mult).then_inc(o_ready, 1)

            moments_of(0)
            normalise(0, True)
            for kind, n in FIRST_JOBS[:-1]:
                take(kind, n, 0)
            copy_adj(0)
            for hh in range(2):
                shift(0, hh, True)

            def body(b, first, last):
                for hh in range(HEADS):
                    if hh + 2 < HEADS:
                        shift(b, hh + 2, first and hh + 2 < 4)
                    elif not last:
                        if hh + 2 == HEADS:
                            copy_adj(b + 1)
                        shift(b + 1, hh + 2 - HEADS, False)
                    pair = (b, hh // 2 - 1) if hh >= 2 else None if first else (b - 1, PAIRS - 1)
                    if pair and hh % 2:
                        divide4(*pair)
                    elif pair:
                        divide1(*pair)
                    for kind, n, d in ended_before(hh, first, last):
                        take(kind, n, b + d)
                    if pair and hh % 2 == 0:
                        divide2(*pair)
                    low_probs(b, hh, first and hh < 2)
                    if pair and hh % 2 == 0:
                        divide3(*pair)
                    if not last and hh == 1:
                        moments_of(b + 1)
                    if not last and hh == 3:
                        normalise(b + 1, False)

            body(0, True, False)
            with dve.Fori(1, B - 1) as b:
                body(b, False, False)
            body(B - 1, False, True)
            take("o", 2, B - 1)
            for divide in (divide1, divide2, divide3, divide4):
                divide(B - 1, PAIRS - 1)
            take("o", 3, B - 1)
            for n in range(NT):
                take("y", n, B - 1)

        @block.gpsimd
        def _(pool):
            nc.gpsimd.memset(ident[:, :], 0.0).then_inc(ident_zero, 1)
            pool.wait_ge(ident_zero, 1)
            nc.gpsimd.affine_select(out=ident[:, :], in_=ident[:, :], compare_op=ALU.not_equal, fill=1.0, base=0,
                                    pattern=[[-1, P]], channel_multiplier=1).then_inc(constants, 1)
            nc.gpsimd.memset(minus_half[:, :], -0.5).then_inc(constants, 1)
            nc.gpsimd.memset(v_parts[:, :, :, ONES:LOW], 1.0).then_inc(constants, 1)

            def deviations(b):
                pool.wait_ge(moments, b + 1)
                settled(pool, "pool")
                nc.gpsimd.tensor_scalar(var_eps[:, :], mean_var[:, :, 1], EPS, None, ALU.add).then_inc(eps_added, 1)
                pool.wait_ge(eps_added, b + 1)
                nc.gpsimd.tensor_tensor(rstd[:, :], var_eps[:, :], minus_half[:, :], ALU.pow).then_inc(rstd_ready, 1)

            def fold(b, pair, early):
                src = minus[pair % 2][:, :, :, :].rearrange("p h t n -> p (h t) n")
                f1, f2, f3 = fold1[pair % 2], fold2[pair % 2], fold3[pair % 2]
                pool.wait_ge(shifted, head_no(b, 2 * pair + 2))
                nc.gpsimd.tensor_tensor(f1[:, :, :], src[:, :, 0:N // 2], src[:, :, N // 2:N],
                                        ALU.add).then_inc(folded1, 1)
                pool.wait_ge(folded1, b * PAIRS + (pair + 1))
                nc.gpsimd.tensor_tensor(f2[:, :, :], f1[:, :, 0:N // 4], f1[:, :, N // 4:N // 2],
                                        ALU.add).then_inc(folded2, 1)
                pool.wait_ge(folded2, b * PAIRS + (pair + 1))
                if not early:
                    pool.wait_ge(some_ready, b * PAIRS + (pair - 1))
                nc.gpsimd.tensor_tensor(f3[:, :, :], f2[:, :, 0:N // 8], f2[:, :, N // 8:N // 4],
                                        ALU.add).then_inc(folded3, 1)

            deviations(0)
            fold(0, 0, True)

            def body(b, first, last):
                for hh in range(HEADS):
                    if not last and hh == 1:
                        deviations(b + 1)
                    if hh % 2 == 1:
                        if hh + 2 < HEADS:
                            fold(b, hh // 2 + 1, first and hh // 2 + 1 < 2)
                        elif not last:
                            fold(b + 1, 0, False)

            body(0, True, False)
            with pool.Fori(1, B - 1) as b:
                body(b, False, False)
            body(B - 1, False, True)


_OUT = (32, 256, 512)


def kernel(x, adj, L0_gnn_Wq, L0_gnn_Wk, L0_gnn_Wv, L0_gnn_Wo):
    import numpy as np
    import concourse.bacc as bacc
    from concourse import mybir
    from concourse.bass_utils import run_bass_kernel_spmd

    laid_out = {
        "x": np.ascontiguousarray(x),
        "adj": np.ascontiguousarray(adj),
        "wq_t": np.ascontiguousarray(np.asarray(L0_gnn_Wq).T),
        "wk_t": np.ascontiguousarray(np.asarray(L0_gnn_Wk).T),
        "wv": np.ascontiguousarray(L0_gnn_Wv),
        "wo_t": np.ascontiguousarray(np.asarray(L0_gnn_Wo).T),
    }
    nc = bacc.Bacc("TRN2", target_bir_lowering=False, num_devices=1)
    args = [nc.dram_tensor(name, a.shape, mybir.dt.from_np(a.dtype), kind="ExternalInput").ap()
            for name, a in laid_out.items()]
    out = nc.dram_tensor("out", _OUT, mybir.dt.float32, kind="ExternalOutput").ap()
    attention_block(nc, *args, out)
    got = run_bass_kernel_spmd(nc, [laid_out], core_ids=[0])
    return got.results[0]["out"]
```

```python
from contextlib import ExitStack

import concourse.bass as bass
from concourse import mybir

ALU = mybir.AluOpType
ACT = mybir.ActivationFunctionType
AX_X = mybir.AxisListType.X
F32 = mybir.dt.float32
F32R = mybir.dt.float32r
F16 = mybir.dt.float16
I32 = mybir.dt.int32

P = 128
HEADS = 16
EPS = 1e-5
GREATEST = 3.4e38
EXPONENT = 0x7F800000
LEAST_SCALE = 2.0 ** -100

PRODUCTS = {"qk": 24, "v": 12, "y": 12, "h": 1, "o": 1}
JOBS = {
    0: [("qk", 3, 0, 0, 12)],
    1: [("qk", 3, 0, 12, 24), ("v", 2, 0, 0, 2)],
    2: [("v", 2, 0, 2, 12), ("v", 3, 0, 0, 3)],
    3: [("v", 3, 0, 3, 12), ("o", 1, -1, 0, 1)],
    4: [("h", 0, 1, 0, 1), ("y", 0, -1, 0, 6)],
    5: [("y", 0, -1, 6, 9), ("h", 1, 1, 0, 1), ("y", 0, -1, 9, 12)],
    6: [("qk", 0, 1, 0, 12)],
    7: [("qk", 0, 1, 12, 24)],
    8: [("qk", 1, 1, 0, 12)],
    9: [("qk", 1, 1, 12, 24)],
    10: [("qk", 2, 1, 0, 12)],
    11: [("qk", 2, 1, 12, 24)],
    12: [("y", 1, -1, 0, 6)],
    13: [("y", 1, -1, 6, 12), ("o", 0, 0, 0, 1)],
    14: [("v", 0, 1, 0, 12)],
    15: [("v", 1, 1, 0, 12)],
}
ORDER = [j[:2] for hh in range(HEADS) for j in JOBS[hh] if j[3] == 0]
BANK = {job: i % 2 for i, job in enumerate(ORDER)}
LAST_JOBS = {15: [("y", 0, 0, 0, 6), ("y", 1, 0, 0, 6)]}
PER_BATCH = {"h": 2, "qk": 4, "v": 4, "o": 2, "y": 2}
AHEAD = 3
SCORE_BANK = [hh % 3 for hh in range(HEADS - 1)] + [1]


def bank_before(hh):
    return next(n for n in range(1, HEADS) if SCORE_BANK[hh - n] == SCORE_BANK[hh])


def jobs_at(hh, first, last):
    here = [j for j in JOBS[hh] if not (first and j[2] < 0) and not (last and j[2] > 0)]
    return here + (LAST_JOBS.get(hh, []) if last else [])


def ended_before(hh, first, last):
    if hh:
        return [j[:3] for j in jobs_at(hh - 1, first, last) if j[4] == PRODUCTS[j[0]]]
    return [(kind, n, d - 1) for kind, n, d, _, end in JOBS[HEADS - 1]
            if end == PRODUCTS[kind] and not (first and d < 1)]


def attention_block(nc, x, adj, wq_t, wk_t, wv, wo_t, out):
    B, N, D = x.shape
    NT = N // P
    KT = D // P
    HD = D // HEADS
    G = P // HD
    HALF = D // 2
    HH = HEADS // 2
    VW = 2 * HD + 2
    ONES, LOW = HD, HD + 1
    PAIRS = HEADS // 2
    HALF_SCALE = 0.5 * float(D) ** -0.5
    STACKED = 16 * 3
    assert NT == 2 and KT == 4 and G == 4 and HD == 32

    x_d = x.rearrange("b (t p) d -> b p t d", p=P)
    adj_d = adj.rearrange("b (t p) m -> b p t m", p=P)
    out_d = out.rearrange("b (t p) d -> b p t d", p=P)

    with ExitStack() as ctx:
        def sb(name, shape, dt=F32):
            return ctx.enter_context(nc.sbuf_tensor(name, shape, dt))

        def psum(name):
            return ctx.enter_context(nc.psum_tensor(name, [P, 512], F32))

        def sem(name):
            return ctx.enter_context(nc.semaphore(name))

        w_hi = [sb(f"w_hi{i}", [P, KT, D], F32R) for i in range(4)]
        w_lo = [sb(f"w_lo{i}", [P, KT, D], F32R) for i in range(4)]
        WQ, WK, WV, WO = range(4)
        HIGHS = [(i, half) for i in (WQ, WK, WV, WO) for half in range(2)]
        DVE_LOWS = [(WQ, 0), (WQ, 1), (WK, 0), (WV, 0), (WV, 1)]
        POOL_LOWS = [(WK, 1), (WO, 0), (WO, 1)]
        x_in = sb("x_in", [P, NT, D])
        x_res = sb("x_res", [P, NT, D])
        h = sb("h", [P, NT, D])
        y = sb("y", [P, NT, D])
        hT_hi = sb("hT_hi", [P, KT, N], F32R)
        hT_lo = sb("hT_lo", [P, KT, N], F32R)
        qk_parts = sb("qk_parts", [P, 2, 4, 2, N], F32R)
        qk_stack = sb("qk_stack", [3 * HD, 2, G, 2, 2, N], F32R)
        v_parts = sb("v_parts", [P, NT, HEADS, VW], F16)
        adj_in = sb("adj_in", [P, NT, N])
        adj_now = sb("adj_now", [P, NT, N])
        minus = [sb(f"minus{i}", [P, 2, NT, N]) for i in range(2)]
        minus_max = sb("minus_max", [P, 4, 2, NT])
        fold1 = [sb(f"fold1_{i}", [P, 2 * NT, N // 2]) for i in range(2)]
        fold2 = [sb(f"fold2_{i}", [P, 2 * NT, N // 4]) for i in range(2)]
        fold3 = [sb(f"fold3_{i}", [P, 2 * NT, N // 8]) for i in range(2)]
        some = [sb(f"some{i}", [P, 4, 2 * NT]) for i in range(2)]
        o_raw = [sb(f"o_raw{i}", [P, 2 * NT, VW - 1]) for i in range(2)]
        probs = [sb(f"probs{i}", [P, NT, N]) for i in range(2)]
        pT_hi = [sb(f"pT_hi{i}", [P, NT, N], F16) for i in range(4)]
        pT_lo = [sb(f"pT_lo{i}", [P, NT, N], F16) for i in range(4)]
        o = sb("o", [P, NT, D])
        oT_hi = sb("oT_hi", [P, KT, N], F32R)
        oT_lo = sb("oT_lo", [P, KT, N], F32R)
        v_scale = sb("v_scale", [P, 4, KT])
        w_in = [[m[:, :, :, :].rearrange("p a b n -> p (a b n)").rearrange("p (k n) -> p k n", k=2) for m in minus],
                [y[:, :, :], x_res[:, :, :]],
                [qk_parts[:, 1, 2 * i:2 * i + 2, :, :].bitcast(F32).rearrange("p a g n -> p a (g n)")
                 for i in range(2)],
                [o[:, :, :], sb("w_in2", [P, 2, D])[:, :, :]]]
        stats = sb("stats", [P, NT, 6])
        mean_var = sb("mean_var", [P, NT, 2])
        var_eps = sb("var_eps", [P, NT])
        minus_mean = sb("minus_mean", [P, NT])
        minus_half = sb("minus_half", [P, NT])
        rstd = sb("rstd", [P, NT])
        ident = sb("ident", [P, P])

        s_ps = [psum(f"s_ps{i}") for i in range(3)]
        pT_ps = [psum(f"pT_ps{i}") for i in range(2)]
        o_ps = psum("o_ps")
        job_ps = [psum(f"job_ps{i}") for i in range(2)] + [s_ps[0]]
        v_ps = [pT_ps, s_ps]

        w_loaded = [[sem(f"w_loaded{i}_{half}") for half in range(2)] for i in range(4)]
        w_high = sem("w_high")
        w_split, w_split_pool = sem("w_split"), sem("w_split_pool")
        ident_zero, constants = sem("ident_zero"), sem("constants")
        x_loaded, adj_loaded, res_loaded = sem("x_loaded"), sem("adj_loaded"), sem("res_loaded")
        adj_copied = sem("adj_copied")
        stats_done, moments = sem("stats_done"), sem("moments")
        mean_turned, eps_added = sem("mean_turned"), sem("eps_added")
        rstd_ready, h_ready = sem("rstd_ready"), sem("h_ready")
        ended = {k: sem(f"ended_{k}") for k in PER_BATCH}
        high = {k: sem(f"high_{k}") for k in PER_BATCH if k != "y"}
        taken = {k: sem(f"taken_{k}") for k in PER_BATCH}
        v_extent = sem("v_extent")
        v_scaled, v_turned, scale_ready = sem("v_scaled"), sem("v_turned"), sem("scale_ready")
        o_scaled = sem("o_scaled")
        stacked = [sem(f"stacked{j}") for j in range(G)]
        scores_ready, shifted, exp_done = sem("scores_ready"), sem("shifted"), sem("exp_done")
        pT_ready, pT_high, pT_split = sem("pT_ready"), sem("pT_high"), sem("pT_split")
        pv_done, folded1 = sem("pv_done"), sem("folded1")
        folded2, folded3 = sem("folded2"), sem("folded3")
        some_ready, keep_ready = sem("some_ready"), sem("keep_ready")
        rcp_ready, factor_ready, o_ready = sem("rcp_ready"), sem("factor_ready"), sem("o_ready")
        o_added = sem("o_added")
        o_copied, y_ready = sem("o_copied"), sem("y_ready")
        stored = [sem(f"stored{i}") for i in range(NT)]

        went_on = {e: sem(f"went_on_{e}") for e in ("dve", "pool", "sp")}

        block = ctx.enter_context(nc.Block())

        def settled(engine, name):
            engine.sem_inc(went_on[name], 1)

        def split_waits(engine, halves):
            for done, order in ((w_split, DVE_LOWS), (w_split_pool, POOL_LOWS)):
                here = [order.index(w) + 1 for w in halves if w in order]
                if here:
                    engine.wait_ge(done, max(here))

        def bank(kind, n, b):
            if isinstance(b, int) and (kind, n, b) == ("h", 1, 0):
                return 1 - BANK[kind, n]
            if isinstance(b, int) and (kind, n, b) == ("o", 1, B - 1):
                return 2
            return BANK[kind, n]

        def count(kind, n, b):
            return b * PER_BATCH[kind] + (n + 1)

        def head_no(b, hh):
            return b * HEADS + hh

        def stack_count(half, b):
            return b * (2 * STACKED) + STACKED * (half + 1)

        @block.sync
        def _(sp):
            def stack(half, b, first):
                sp.wait_ge(taken["qk"], count("qk", 2 * half + 1, b))
                settled(sp, "sp")
                if not first:
                    sp.wait_ge(scores_ready, head_no(b, 0) + (HH * (half + 1) - HEADS))
                    settled(sp, "sp")
                for j in range(G):
                    for r, pair in enumerate((slice(1, 3), slice(0, 3, 2), slice(1, 4, 2))):
                        sp.dma_start(qk_stack[HD * r:HD * (r + 1), half, j, :, :, :].bitcast(F32),
                                     qk_parts[HD * j:HD * (j + 1), half, pair, :, :].bitcast(F32)
                                     ).then_inc(stacked[j], 16)

            def load_tokens(b):
                sp.wait_ge(h_ready, b)
                settled(sp, "sp")
                sp.dma_start(x_in[:, :, :], x_d[b]).then_inc(x_loaded, 16)

            sp.dma_start(x_in[:, :, :], x_d[0]).then_inc(x_loaded, 16)
            for i, w in ((WQ, wq_t), (WK, wk_t), (WV, wv), (WO, wo_t)):
                for half in range(2):
                    sp.dma_start(w_in[i][half], w.rearrange("(k p) n -> p k n", p=P)[:, 2 * half:2 * half + 2, :]
                                 ).then_inc(w_loaded[i][half], 16)
            sp.dma_start(adj_in[:, :, :], adj_d[0]).then_inc(adj_loaded, 16)
            split_waits(sp, [(WK, 1)])
            sp.dma_start(x_res[:, :, :], x_d[0]).then_inc(res_loaded, 16)
            load_tokens(1)
            stack(0, 0, True)

            def body(b, first, last):
                if not last:
                    sp.wait_ge(adj_copied, b + 1)
                    settled(sp, "sp")
                    sp.dma_start(adj_in[:, :, :], adj_d[b + 1]).then_inc(adj_loaded, 16)
                stack(1, b, first)
                if not (last or isinstance(b, int) and b + 2 == B):
                    load_tokens(b + 2)
                if not first:
                    store(b - 1, 0)
                if not last:
                    stack(0, b + 1, False)
                if not first:
                    store(b - 1, 1)
                    sp.dma_start(x_res[:, :, :], x_d[b]).then_inc(res_loaded, 16)

            def store(b, t):
                sp.wait_ge(y_ready, b * NT + (t + 1))
                settled(sp, "sp")
                sp.dma_start(out_d[b, :, t, :], y[:, t, :]).then_inc(stored[t], 16)

            body(0, True, False)
            with sp.Fori(1, B - 2) as b:
                body(b, False, False)
            body(B - 2, False, False)
            body(B - 1, False, True)
            for t in range(NT):
                store(B - 1, t)
            for t in range(NT):
                sp.wait_ge(stored[t], 16 * B)

        @block.tensor
        def _(pe):
            last_in = {}

            def begin(kind, n, d, b):
                i = bank(kind, n, b + d)
                if i in last_in:
                    was, m, e = last_in[i]
                    pe.wait_ge(taken[was], count(was, m, b + e))
                last_in[i] = (kind, n, d)

            def product(dst, lhs, rhs, start, stop):
                terms = [(k, a, c) for k in range(KT) for a, c in ((0, 0), (0, 1), (1, 0))]
                for i in range(max(start, 0), min(stop, len(terms))):
                    k, a, c = terms[i]
                    end = nc.tensor.matmul(dst, lhs[a](k), rhs[c](k), start=i == 0, stop=i == len(terms) - 1)
                return end

            hT = (hT_hi, hT_lo)
            oT = (oT_hi, oT_lo)

            def job(kind, n, d, start, stop, b):
                ps = job_ps[bank(kind, n, b + d)]
                if start == 0:
                    begin(kind, n, d, b)
                if kind == "h":
                    if n == 0:
                        pe.wait_ge(h_ready, b + (d + 1))
                    for k in range(2):
                        for t in range(NT):
                            end = nc.tensor.transpose(ps[:, k * N + t * P:k * N + (t + 1) * P],
                                                      h[:, t, (2 * n + k) * P:(2 * n + k + 1) * P], ident[:, :])
                elif kind == "qk":
                    if n == 0 and start == 0:
                        pe.wait_ge(taken["h"], count("h", 1, b + d))
                    half = PRODUCTS["qk"] // 2
                    for i, w in enumerate((WQ, WK)):
                        if start < (i + 1) * half and stop > i * half:
                            end = product(ps[:, i * N:(i + 1) * N],
                                          [lambda k, w=m: w[:, k, n * P:(n + 1) * P] for m in (w_hi[w], w_lo[w])],
                                          [lambda k, v=v: v[:, k, :] for v in hT], start - i * half, stop - i * half)
                elif kind == "v":
                    t, half = n % NT, n // NT
                    end = product(ps[:, 0:HALF], [lambda k, v=v: v[:, k, t * P:(t + 1) * P] for v in hT],
                                  [lambda k, w=w: w[:, k, half * HALF:(half + 1) * HALF] for w in (w_hi[WV], w_lo[WV])],
                                  start, stop)
                elif kind == "o":
                    pe.wait_ge(o_ready, (b + d) * PAIRS + 4 * (n + 1))
                    for k in range(2):
                        for t in range(NT):
                            end = nc.tensor.transpose(ps[:, k * N + t * P:k * N + (t + 1) * P],
                                                      o[:, t, (2 * n + k) * P:(2 * n + k + 1) * P], ident[:, :])
                else:
                    half = PRODUCTS["y"] // 2
                    if n == 0 and start == 0:
                        pe.wait_ge(taken["o"], count("o", 0, b + d))
                    if n == 0 and start <= half < stop:
                        pe.wait_ge(taken["o"], count("o", 1, b + d))
                    end = product(ps[:, :], [lambda k, v=v: v[:, k, n * P:(n + 1) * P] for v in oT],
                                  [lambda k, w=w: w[:, k, :] for w in (w_hi[WO], w_lo[WO])], start, stop)
                if stop == PRODUCTS[kind]:
                    end.then_inc(ended[kind], 1)

            def scores(b, hh, early=False):
                if hh % HH < G:
                    pe.wait_ge(stacked[hh % G], stack_count(hh // HH, b))
                if not early:
                    pe.wait_ge(shifted, head_no(b, hh) + (1 - bank_before(hh)))
                stack = qk_stack[:, hh // HH, hh % G, :, hh % HH // G, :]
                for t in range(NT):
                    end = nc.tensor.matmul(s_ps[SCORE_BANK[hh]][:, t * N:(t + 1) * N], stack[:, 0, t * P:(t + 1) * P],
                                           stack[:, 1, :], start=True, stop=True)
                end.then_inc(scores_ready, 1)

            def transpose_probs(b, hh, early):
                pe.wait_ge(exp_done, head_no(b, hh) + 1)
                if not early:
                    pe.wait_ge(pT_split, head_no(b, hh) - 1)
                for m in range(NT):
                    for t in range(NT):
                        end = nc.tensor.transpose(pT_ps[hh % 2][:, m * N + t * P:m * N + (t + 1) * P],
                                                  probs[hh % 2][:, t, m * P:(m + 1) * P], ident[:, :])
                end.then_inc(pT_ready, 1)

            def values(b, hh, early):
                if hh % HH == 0:
                    pe.wait_ge(taken["v"], count("v", 2 * (hh // HH) + 1, b))
                if hh % 2 == 0 and not early:
                    pe.wait_ge(o_copied, b * PAIRS + hh // 2)
                pe.wait_ge(pT_split, head_no(b, hh) + 1)
                for t in range(NT):
                    q = (hh % 2) * NT + t
                    ps = o_ps[:, q * P:(q + 1) * P]
                    for m in range(NT):
                        hi = pT_hi[hh % 4][:, m, t * P:(t + 1) * P]
                        lo = pT_lo[hh % 4][:, m, t * P:(t + 1) * P]
                        v = v_parts[:, m, hh, :]
                        nc.tensor.matmul(ps[:, 0:LOW + HD], hi, v[:, 0:LOW + HD], start=m == 0, stop=False)
                        end = nc.tensor.matmul(ps[:, 0:HD + 1], lo, v[:, 0:HD + 1], start=False, stop=m == NT - 1)
                end.then_inc(pv_done, 1)

            def turn(half):
                pe.wait_ge(v_scaled, half + 1)
                for k in range(KT):
                    for t in range(2):
                        col = (k % 2) * HALF + t * P
                        end = nc.tensor.transpose(v_ps[half][k // 2][:, col:col + P],
                                                  w_in[WV][half][:, t, k * P:(k + 1) * P], ident[:, :])
                end.then_inc(v_turned, 1)

            pe.wait_ge(constants, 3)
            for n in range(2):
                job("h", n, 0, 0, 1, 0)
            split_waits(pe, [(WQ, 1)])
            job("qk", 0, 0, 0, 12, 0)
            split_waits(pe, [(WK, 0), (WK, 1)])
            job("qk", 0, 0, 12, 24, 0)
            job("qk", 1, 0, 0, 24, 0)
            for half in range(2):
                turn(half)
            job("qk", 2, 0, 0, 24, 0)
            split_waits(pe, [(WV, 1)])
            for n in range(2):
                job("v", n, 0, 0, 12, 0)
            for hh in range(AHEAD):
                scores(0, hh, True)

            def body(b, first, last):
                for hh in range(HEADS):
                    transpose_probs(b, hh, first and hh < 2)
                    if hh + AHEAD < HEADS:
                        scores(b, hh + AHEAD)
                    elif not last:
                        scores(b + 1, hh + AHEAD - HEADS)
                    for was in range(hh - 2, hh) if hh % 2 == 0 else ():
                        if was >= 0:
                            values(b, was, first and was < 2)
                        elif not first:
                            values(b - 1, HEADS + was, False)
                    for kind, n, d, start, stop in jobs_at(hh, first, last):
                        job(kind, n, d, start, stop, b)
                for i, (kind, n, d) in last_in.items():
                    last_in[i] = (kind, n, d - 1)

            body(0, True, False)
            split_waits(pe, [(WO, 1)])
            with pe.Fori(1, B - 1) as b:
                body(b, False, False)
            body(B - 1, False, True)
            for hh in range(HEADS - 2, HEADS):
                values(B - 1, hh, False)
            job("o", 1, -1, 0, 1, B)
            for n in range(NT):
                job("y", n, -1, 6, 12, B)

        @block.scalar
        def _(act):
            def high_weight(i, half):
                if i == WV:
                    act.wait_ge(v_turned, half + 1)
                    for j in range(2):
                        end = nc.scalar.activation(w_hi[WV][:, 2 * j:2 * j + 2, half * HALF:(half + 1) * HALF],
                                                   v_ps[half][j][:, :].rearrange("p (k n) -> p k n", k=2), ACT.Copy)
                    end.then_inc(w_high, 1)
                else:
                    if i == WO:
                        act.wait_ge(o_scaled, half + 1)
                    else:
                        act.wait_ge(w_loaded[i][half], 16)
                    nc.scalar.activation(w_hi[i][:, 2 * half:2 * half + 2, :], w_in[i][half],
                                         ACT.Copy).then_inc(w_high, 1)

            def take(kind, n, b, early=False):
                ps = job_ps[bank(kind, n, b)]
                if kind == "y" and not (isinstance(b, int) and b == 0):
                    act.wait_ge(stored[n], b * 16)
                act.wait_ge(ended[kind], count(kind, n, b))
                if kind == "h":
                    nc.scalar.activation(hT_hi[:, 2 * n:2 * n + 2, :], ps[:, :].rearrange("p (k n) -> p k n", k=2),
                                         ACT.Relu).then_inc(high["h"], 1)
                elif kind == "qk":
                    nc.scalar.activation(qk_parts[:, n // 2, 1, n % 2, :], ps[:, 0:N], ACT.Copy, scale=HALF_SCALE)
                    nc.scalar.activation(qk_parts[:, n // 2, 2, n % 2, :], ps[:, N:2 * N],
                                         ACT.Copy).then_inc(high["qk"], 1)
                elif kind == "v":
                    t, half = n % NT, n // NT
                    if not early:
                        act.wait_ge(pv_done, head_no(b, 0) + (HH * (half + 1) - HEADS))
                    nc.scalar.activation(v_parts[:, t, half * HH:(half + 1) * HH, 0:HD],
                                         ps[:, 0:HALF].rearrange("p (h d) -> p h d", d=HD),
                                         ACT.Copy).then_inc(high["v"], 1)
                elif kind == "o":
                    nc.scalar.activation(oT_hi[:, 2 * n:2 * n + 2, :], ps[:, :].rearrange("p (k n) -> p k n", k=2),
                                         ACT.Copy).then_inc(high["o"], 1)
                else:
                    nc.scalar.activation(y[:, n, :], ps[:, :], ACT.Copy).then_inc(taken["y"], 1)

            def copy_outputs(b, pair, early):
                act.wait_ge(pv_done, head_no(b, 2 * pair + 2))
                if not early:
                    act.wait_ge(o_ready, b * PAIRS + (pair - 1))
                nc.scalar.activation(o_raw[pair % 2][:, :, :],
                                     o_ps[:, :].rearrange("p (q c) -> p q c", c=P)[:, :, 0:LOW + HD],
                                     ACT.Copy).then_inc(o_copied, 1)

            def exponentials(b, hh, early):
                act.wait_ge(shifted, head_no(b, hh) + 1)
                if not early:
                    act.wait_ge(pT_ready, head_no(b, hh) - 1)
                for t in range(NT):
                    end = nc.scalar.activation(probs[hh % 2][:, t, :], minus[hh // 2 % 2][:, hh % 2, t, :], ACT.Exp,
                                               bias=minus_max[:, hh // 2 % 4, hh % 2, t:t + 1], scale=-1.0)
                end.then_inc(exp_done, 1)

            def high_probs(b, hh, early):
                act.wait_ge(pT_ready, head_no(b, hh) + 1)
                if not early:
                    act.wait_ge(pv_done, head_no(b, hh) - 3)
                nc.scalar.activation(pT_hi[hh % 4][:, :, :], pT_ps[hh % 2][:, :].rearrange("p (m n) -> p m n", m=NT),
                                     ACT.Copy).then_inc(pT_high, 1)

            for half in range(2):
                high_weight(WQ, half)
            high_weight(WK, 0)
            for n in range(2):
                take("h", n, 0)
            high_weight(WK, 1)
            for n in range(2):
                take("qk", n, 0, True)
            for half in range(2):
                high_weight(WV, half)
            high_weight(WO, 0)
            take("qk", 2, 0, True)
            high_weight(WO, 1)
            take("v", 0, 0, True)
            exponentials(0, 0, True)

            def body(b, first, last):
                for hh in range(HEADS):
                    if hh % 2:
                        if hh > 1:
                            copy_outputs(b, hh // 2 - 1, first and hh < 7)
                        elif not first:
                            copy_outputs(b - 1, PAIRS - 1, False)
                    if hh + 1 < HEADS:
                        exponentials(b, hh + 1, first and hh + 1 < 2)
                    elif not last:
                        exponentials(b + 1, 0, False)
                    for kind, n, d in ended_before(hh, first, last):
                        take(kind, n, b + d, first and (kind, d) in (("v", 0), ("qk", 0)))
                    high_probs(b, hh, first and hh < 4)

            body(0, True, False)
            with act.Fori(1, B - 1) as b:
                body(b, False, False)
            body(B - 1, False, True)
            copy_outputs(B - 1, PAIRS - 1, False)
            take("o", 1, B - 1)
            for n in range(NT):
                take("y", n, B - 1)

        @block.vector
        def _(dve):
            def moments_of(b):
                dve.wait_ge(x_loaded, (b + 1) * 16)
                for t in range(NT):
                    end = nc.vector.bn_stats(stats[:, t, :], x_in[:, t, :])
                end.then_inc(stats_done, 1)
                dve.wait_ge(stats_done, b + 1)
                settled(dve, "dve")
                for t in range(NT):
                    end = nc.vector.bn_aggr(mean_var[:, t, :], stats[:, t, :])
                end.then_inc(moments, 1)

            def scale_values(half):
                part = slice(2 * half, 2 * half + 2)
                w = w_in[WV][half]
                dve.wait_ge(w_loaded[WV][half], 16)
                nc.vector.tensor_reduce(v_scale[:, 0, part], w, AX_X, ALU.max)
                nc.vector.tensor_reduce(v_scale[:, 1, part], w, AX_X, ALU.min).then_inc(v_extent, 1)
                dve.wait_ge(v_extent, 5 * half + 1)
                nc.vector.scalar_tensor_tensor(v_scale[:, 2, part], v_scale[:, 1, part], -1.0, v_scale[:, 0, part],
                                               ALU.mult, ALU.max).then_inc(v_extent, 1)
                dve.wait_ge(v_extent, 5 * half + 2)
                nc.vector.tensor_scalar(v_scale[:, 3, part], v_scale[:, 2, part], LEAST_SCALE, None,
                                        ALU.max).then_inc(v_extent, 1)
                dve.wait_ge(v_extent, 5 * half + 3)
                nc.vector.tensor_scalar(v_scale[:, 2, part].bitcast(I32), v_scale[:, 3, part].bitcast(I32),
                                        EXPONENT, None, ALU.bitwise_and).then_inc(v_extent, 1)
                dve.wait_ge(v_extent, 5 * half + 4)
                nc.vector.reciprocal(v_scale[:, 3, part], v_scale[:, 2, part]).then_inc(v_extent, 1)
                dve.wait_ge(v_extent, 5 * half + 5)
                for k in range(2):
                    end = nc.vector.tensor_scalar(w[:, k, :], w[:, k, :],
                                                  v_scale[:, 3, 2 * half + k:2 * half + k + 1], None, ALU.mult)
                end.then_inc(v_scaled, 1)

            def low_weight(i, half):
                dve.wait_ge(w_high, HIGHS.index((i, half)) + 1)
                if i == WV:
                    for j in range(2):
                        cols = slice(half * HALF, (half + 1) * HALF)
                        end = nc.vector.tensor_tensor(
                            w_lo[WV][:, 2 * j:2 * j + 2, cols],
                            v_ps[half][j][:, :].rearrange("p (k n) -> p k n", k=2),
                            w_hi[WV][:, 2 * j:2 * j + 2, cols].bitcast(F32), ALU.subtract)
                else:
                    end = nc.vector.tensor_tensor(w_lo[i][:, 2 * half:2 * half + 2, :], w_in[i][half],
                                                  w_hi[i][:, 2 * half:2 * half + 2, :].bitcast(F32), ALU.subtract)
                end.then_inc(w_split, 1)

            def take(kind, n, b):
                if kind == "y":
                    return
                ps = job_ps[bank(kind, n, b)]
                dve.wait_ge(high[kind], count(kind, n, b))
                if kind == "h":
                    nc.vector.scalar_tensor_tensor(hT_lo[:, 2 * n:2 * n + 2, :].rearrange("p k n -> p (k n)"),
                                                   ps[:, :], 0.0,
                                                   hT_hi[:, 2 * n:2 * n + 2, :].bitcast(F32).rearrange("p k n -> p (k n)"),
                                                   ALU.max, ALU.subtract).then_inc(taken["h"], 1)
                elif kind == "qk":
                    parts = qk_parts[:, n // 2, :, n % 2, :]
                    nc.vector.scalar_tensor_tensor(parts[:, 0, :], ps[:, 0:N], HALF_SCALE,
                                                   parts[:, 1, :].bitcast(F32), ALU.mult, ALU.subtract)
                    nc.vector.tensor_tensor(parts[:, 3, :], ps[:, N:2 * N], parts[:, 2, :].bitcast(F32),
                                            ALU.subtract).then_inc(taken["qk"], 1)
                elif kind == "v":
                    t, half = n % NT, n // NT
                    part = v_parts[:, t, half * HH:(half + 1) * HH, :]
                    nc.vector.tensor_tensor(part[:, :, LOW:LOW + HD],
                                            ps[:, 0:HALF].rearrange("p (h d) -> p h d", d=HD), part[:, :, 0:HD],
                                            ALU.subtract).then_inc(taken["v"], 1)
                elif kind == "o":
                    nc.vector.tensor_tensor(oT_lo[:, 2 * n:2 * n + 2, :], ps[:, :].rearrange("p (k n) -> p k n", k=2),
                                            oT_hi[:, 2 * n:2 * n + 2, :].bitcast(F32), ALU.subtract).then_inc(taken["o"], 1)

            def shift(b, hh, early):
                pair = hh // 2
                if hh % 2 == 0 and not early:
                    dve.wait_ge(folded1, b * PAIRS + (pair - 1))
                    dve.wait_ge(exp_done, head_no(b, hh) - 2)
                dve.wait_ge(scores_ready, head_no(b, hh) + 1)
                settled(dve, "dve")
                for t in range(NT):
                    end = nc.vector.tensor_tensor_reduce(
                        out=minus[pair % 2][:, hh % 2, t, :], in0=s_ps[SCORE_BANK[hh]][:, t * N:(t + 1) * N],
                        in1=adj_now[:, t, :], scale=-2.0, scalar=GREATEST, op0=ALU.add, op1=ALU.min,
                        accum_out=minus_max[:, pair % 4, hh % 2, t:t + 1])
                end.then_inc(shifted, 1)

            def copy_adj(b):
                dve.wait_ge(adj_loaded, (b + 1) * 16)
                if not (isinstance(b, int) and b == 0):
                    dve.wait_ge(shifted, head_no(b, 0))
                nc.vector.tensor_copy(adj_now[:, :, :], adj_in[:, :, :]).then_inc(adj_copied, 1)
                dve.wait_ge(adj_copied, b + 1)

            def low_probs(b, hh, early):
                dve.wait_ge(pT_high, head_no(b, hh) + 1)
                nc.vector.tensor_tensor(pT_lo[hh % 4][:, :, :], pT_ps[hh % 2][:, :].rearrange("p (m n) -> p m n", m=NT),
                                        pT_hi[hh % 4][:, :, :], ALU.subtract).then_inc(pT_split, 1)

            def factor1(b, pair):
                dve.wait_ge(folded3, b * PAIRS + (pair + 1))
                nc.vector.tensor_reduce(some[pair % 2][:, 0, :], fold3[pair % 2][:, :, :], AX_X,
                                        ALU.add).then_inc(some_ready, 1)
                dve.wait_ge(o_copied, b * PAIRS + (pair + 1))
                nc.vector.reciprocal(some[pair % 2][:, 1, :], o_raw[pair % 2][:, :, ONES]).then_inc(rcp_ready, 1)

            def factor2(b, pair):
                dve.wait_ge(some_ready, b * PAIRS + (pair + 1))
                nc.vector.scalar_tensor_tensor(some[pair % 2][:, 2, :],
                                               minus_max[:, pair % 4, :, :].rearrange("p h t -> p (h t)"), 0.0,
                                               some[pair % 2][:, 0, :], ALU.not_equal, ALU.max).then_inc(keep_ready, 1)

            def factor3(b, pair, early):
                dve.wait_ge(rcp_ready, b * PAIRS + (pair + 1))
                dve.wait_ge(keep_ready, b * PAIRS + (pair + 1))
                if not early:
                    dve.wait_ge(o_ready, b * PAIRS + (pair - 1))
                nc.vector.scalar_tensor_tensor(some[pair % 2][:, 3, :], some[pair % 2][:, 2, :], 0.0,
                                               some[pair % 2][:, 1, :], ALU.not_equal,
                                               ALU.mult).then_inc(factor_ready, 1)

            moments_of(0)
            for half in range(2):
                low_weight(WQ, half)
            for n in range(2):
                take("h", n, 0)
            low_weight(WK, 0)
            for n in range(2):
                scale_values(n)
                take("qk", n, 0)
            for half in range(2):
                low_weight(WV, half)
            take("qk", 2, 0)
            copy_adj(0)
            take("v", 0, 0)
            for hh in range(2):
                shift(0, hh, True)

            def body(b, first, last):
                for hh in range(HEADS):
                    if hh + 2 < HEADS:
                        shift(b, hh + 2, first and hh + 2 < 4)
                    elif not last:
                        if hh + 2 == HEADS:
                            copy_adj(b + 1)
                        shift(b + 1, hh + 2 - HEADS, False)
                    pair = None
                    if hh % 2 and not (first and hh == 1):
                        pair = (b, hh // 2 - 1) if hh > 1 else (b - 1, PAIRS - 1)
                        factor1(*pair)
                    for kind, n, d in ended_before(hh, first, last):
                        take(kind, n, b + d)
                    if pair:
                        factor2(*pair)
                    low_probs(b, hh, first and hh < 2)
                    if pair:
                        factor3(*pair, first and hh < 6)
                    if not last and hh == 0:
                        moments_of(b + 1)

            body(0, True, False)
            with dve.Fori(1, B - 1) as b:
                body(b, False, False)
            body(B - 1, False, True)
            factor1(B - 1, PAIRS - 1)
            factor2(B - 1, PAIRS - 1)
            factor3(B - 1, PAIRS - 1, False)
            take("o", 1, B - 1)

        @block.gpsimd
        def _(pool):
            nc.gpsimd.memset(ident[:, :], 0.0).then_inc(ident_zero, 1)
            pool.wait_ge(ident_zero, 1)
            nc.gpsimd.affine_select(out=ident[:, :], in_=ident[:, :], compare_op=ALU.not_equal, fill=1.0, base=0,
                                    pattern=[[-1, P]], channel_multiplier=1).then_inc(constants, 1)
            nc.gpsimd.memset(minus_half[:, :], -0.5).then_inc(constants, 1)
            nc.gpsimd.memset(v_parts[:, :, :, ONES:LOW], 1.0).then_inc(constants, 1)

            def normalise(b, first):
                pool.wait_ge(moments, b + 1)
                settled(pool, "pool")
                nc.gpsimd.tensor_scalar(minus_mean[:, :], mean_var[:, :, 0], -1.0, None, ALU.mult
                                        ).then_inc(mean_turned, 1)
                nc.gpsimd.tensor_scalar(var_eps[:, :], mean_var[:, :, 1], EPS, None, ALU.add).then_inc(eps_added, 1)
                pool.wait_ge(eps_added, b + 1)
                nc.gpsimd.tensor_tensor(rstd[:, :], var_eps[:, :], minus_half[:, :], ALU.pow).then_inc(rstd_ready, 1)
                pool.wait_ge(rstd_ready, b + 1)
                pool.wait_ge(mean_turned, b + 1)
                if not first:
                    pool.wait_ge(ended["h"], b * 2)
                settled(pool, "pool")
                for t in range(NT):
                    end = nc.gpsimd.tensor_scalar(h[:, t, :], x_in[:, t, :], minus_mean[:, t:t + 1], rstd[:, t:t + 1],
                                                  ALU.add, ALU.mult)
                end.then_inc(h_ready, 1)

            def divide(b, pair):
                pool.wait_ge(factor_ready, b * PAIRS + (pair + 1))
                nc.gpsimd.tensor_tensor(o_raw[pair % 2][:, :, 0:HD], o_raw[pair % 2][:, :, 0:HD],
                                        o_raw[pair % 2][:, :, LOW:LOW + HD], ALU.add).then_inc(o_added, 1)
                pool.wait_ge(o_added, b * PAIRS + (pair + 1))
                col = 2 * pair * HD
                nc.gpsimd.tensor_tensor(
                    o[:, :, col:col + 2 * HD].rearrange("p t (h d) -> p h t d", h=2),
                    o_raw[pair % 2][:, :, 0:HD].rearrange("p (h t) d -> p h t d", h=2),
                    some[pair % 2][:, 3, :].rearrange("p (h t) -> p h t", h=2).unsqueeze(3).to_broadcast([P, 2, NT, HD]),
                    ALU.mult).then_inc(o_ready, 1)

            def residual(b, t):
                if t == 0:
                    pool.wait_ge(res_loaded, (b + 1) * 16)
                pool.wait_ge(taken["y"], count("y", t, b))
                nc.gpsimd.tensor_tensor(y[:, t, :], y[:, t, :], x_res[:, t, :], ALU.add).then_inc(y_ready, 1)

            def fold(b, pair, early):
                src = minus[pair % 2][:, :, :, :].rearrange("p h t n -> p (h t) n")
                f1, f2, f3 = fold1[pair % 2], fold2[pair % 2], fold3[pair % 2]
                pool.wait_ge(shifted, head_no(b, 2 * pair + 2))
                nc.gpsimd.tensor_tensor(f1[:, :, :], src[:, :, 0:N // 2], src[:, :, N // 2:N],
                                        ALU.add).then_inc(folded1, 1)
                pool.wait_ge(folded1, b * PAIRS + (pair + 1))
                nc.gpsimd.tensor_tensor(f2[:, :, :], f1[:, :, 0:N // 4], f1[:, :, N // 4:N // 2],
                                        ALU.add).then_inc(folded2, 1)
                pool.wait_ge(folded2, b * PAIRS + (pair + 1))
                if not early:
                    pool.wait_ge(some_ready, b * PAIRS + (pair - 1))
                nc.gpsimd.tensor_tensor(f3[:, :, :], f2[:, :, 0:N // 8], f2[:, :, N // 8:N // 4],
                                        ALU.add).then_inc(folded3, 1)

            def low_weight(i, half):
                pool.wait_ge(w_high, HIGHS.index((i, half)) + 1)
                nc.gpsimd.tensor_tensor(w_lo[i][:, 2 * half:2 * half + 2, :], w_in[i][half],
                                        w_hi[i][:, 2 * half:2 * half + 2, :].bitcast(F32),
                                        ALU.subtract).then_inc(w_split_pool, 1)

            normalise(0, True)
            low_weight(WK, 1)
            for half in range(2):
                pool.wait_ge(w_loaded[WO][half], 16)
                pool.wait_ge(v_scaled, half + 1)
                for k in range(2):
                    row = w_in[WO][half][:, k, :]
                    end = nc.gpsimd.tensor_scalar(row, row, v_scale[:, 2, 2 * half + k:2 * half + k + 1],
                                                  None, ALU.mult)
                end.then_inc(o_scaled, 1)
            for half in range(2):
                low_weight(WO, half)
            split_waits(pool, [(WO, 1)])
            fold(0, 0, True)

            def body(b, first, last):
                for hh in range(HEADS):
                    if hh % 2 == 1:
                        if hh + 2 < HEADS:
                            fold(b, hh // 2 + 1, first and hh // 2 + 1 < 2)
                        elif not last:
                            fold(b + 1, 0, False)
                        if hh > 1:
                            divide(b, hh // 2 - 1)
                        elif not first:
                            divide(b - 1, PAIRS - 1)
                    if not last and hh == 1:
                        normalise(b + 1, False)
                    for kind, n, d in ended_before(hh, first, last):
                        if kind == "y":
                            residual(b + d, n)

            body(0, True, False)
            with pool.Fori(1, B - 1) as b:
                body(b, False, False)
            body(B - 1, False, True)
            divide(B - 1, PAIRS - 1)
            for t in range(NT):
                residual(B - 1, t)


_OUT = (32, 256, 512)


def kernel(x, adj, L0_gnn_Wq, L0_gnn_Wk, L0_gnn_Wv, L0_gnn_Wo):
    import numpy as np
    import concourse.bacc as bacc
    from concourse import mybir
    from concourse.bass_utils import run_bass_kernel_spmd

    laid_out = {
        "x": np.ascontiguousarray(x),
        "adj": np.ascontiguousarray(adj),
        "wq_t": np.ascontiguousarray(np.asarray(L0_gnn_Wq).T),
        "wk_t": np.ascontiguousarray(np.asarray(L0_gnn_Wk).T),
        "wv": np.ascontiguousarray(L0_gnn_Wv),
        "wo_t": np.ascontiguousarray(np.asarray(L0_gnn_Wo).T),
    }
    nc = bacc.Bacc("TRN2", target_bir_lowering=False, num_devices=1)
    args = [nc.dram_tensor(name, a.shape, mybir.dt.from_np(a.dtype), kind="ExternalInput").ap()
            for name, a in laid_out.items()]
    out = nc.dram_tensor("out", _OUT, mybir.dt.float32, kind="ExternalOutput").ap()
    attention_block(nc, *args, out)
    got = run_bass_kernel_spmd(nc, [laid_out], core_ids=[0])
    return got.results[0]["out"]
```
